# Optimizing a Trainium2 kernel written in Bass

```python
import numpy as np
import jax
import jax.numpy as jnp

def _softmax(x, axis=-1):
    return jax.nn.softmax(x, axis=axis)

def _gelu(x):
    return jax.nn.gelu(x, approximate=True)

def _silu(x):
    return jax.nn.silu(x)

def _sigmoid(x):
    return jax.nn.sigmoid(x)

def _layernorm(x, axis=-1, eps=1e-05):
    m = jnp.mean(x, axis=axis, keepdims=True)
    v = jnp.var(x, axis=axis, keepdims=True)
    return (x - m) / jnp.sqrt(v + eps)

def _scatter_add(tgt, idx, src, axis=0):
    return tgt.at[idx].add(src)

def _segment_sum(src, seg, n):
    return jax.ops.segment_sum(src, seg, n)
kernel_name = 'mk_prb_d1_jaxref_r4_f2e751'

def setup_inputs(seed: int=0):
    np.random.seed(seed)
    _w = jnp.asarray

    def _L0_attn_setup():
        import jax, jax.numpy as jnp
        import numpy as np
        B, S, D_MODEL = (1, 512, 256)
        H = 16
        D = D_MODEL // H
        G = 32
        TOP2, TOP1 = (4, 8)
        WIN = 128
        SCALE = D ** (-0.5)

        def _rotate_half(x):
            x1, x2 = jnp.split(x, 2, axis=-1)
            return jnp.concatenate([-x2, x1], axis=-1)

        def _rope(q, k):
            s = q.shape[2]
            inv_freq = 1.0 / 10000.0 ** (jnp.arange(0, D, 2, dtype=jnp.float32) / D)
            freqs = jnp.arange(s, dtype=jnp.float32)[:, None] * inv_freq[None, :]
            emb = jnp.concatenate([freqs, freqs], axis=-1)
            cos = jnp.cos(emb)[None, None]
            sin = jnp.sin(emb)[None, None]
            return (q * cos + _rotate_half(q) * sin, k * cos + _rotate_half(k) * sin)
        key = jax.random.key(seed)
        ks = jax.random.split(key, 9)
        std = 0.02
        return {'x': jax.random.normal(ks[0], (B, S, D_MODEL), jnp.float32), 'W_q': jax.random.normal(ks[1], (D_MODEL, D_MODEL), jnp.float32) * std, 'W_k': jax.random.normal(ks[2], (D_MODEL, D_MODEL), jnp.float32) * std, 'W_v': jax.random.normal(ks[3], (D_MODEL, D_MODEL), jnp.float32) * std, 'W_o': jax.random.normal(ks[4], (D_MODEL, D_MODEL), jnp.float32) * std, 'k_lod1': jax.random.normal(ks[5], (D, G * D), jnp.float32) * std, 'v_lod1': jax.random.normal(ks[6], (D, G * D), jnp.float32) * std, 'k_lod2': jax.random.normal(ks[7], (D, G * D), jnp.float32) * std, 'v_lod2': jax.random.normal(ks[8], (D, G * D), jnp.float32) * std}
    _L0_attn_in = _L0_attn_setup()

    def _L0_ffn_setup():
        import jax, jax.numpy as jnp
        import numpy as np
        H = 256
        I = 128
        E = 32
        TOP_K = 6
        N_GROUP = 8
        TOPK_GROUP = 4
        SCALE = 2.5
        N_SHARED = 2
        SI = I * N_SHARED
        B, S = (2, 256)
        key = jax.random.key(seed)
        ks = jax.random.split(key, 8)
        x = jax.random.normal(ks[0], (B, S, H), jnp.float32)
        gate_weight = jax.random.normal(ks[1], (E, H), jnp.float32) * 0.02
        e_score_correction_bias = jax.random.normal(ks[2], (E,), jnp.float32) * 0.01
        experts_gate_up = jax.random.normal(ks[3], (E, 2 * I, H), jnp.float32) * 0.02
        experts_down = jax.random.normal(ks[4], (E, H, I), jnp.float32) * 0.02
        shared_gate_w = jax.random.normal(ks[5], (SI, H), jnp.float32) * 0.02
        shared_up_w = jax.random.normal(ks[6], (SI, H), jnp.float32) * 0.02
        shared_down_w = jax.random.normal(ks[7], (H, SI), jnp.float32) * 0.02
        return {'x': x, 'gate_weight': gate_weight, 'e_score_correction_bias': e_score_correction_bias, 'experts_gate_up': experts_gate_up, 'experts_down': experts_down, 'shared_gate_w': shared_gate_w, 'shared_up_w': shared_up_w, 'shared_down_w': shared_down_w}
    _L0_ffn_in = _L0_ffn_setup()
    _d = {'L0_attn_x': _L0_attn_in['x'], 'L0_attn_W_q': _L0_attn_in['W_q'], 'L0_attn_W_k': _L0_attn_in['W_k'], 'L0_attn_W_v': _L0_attn_in['W_v'], 'L0_attn_W_o': _L0_attn_in['W_o'], 'L0_attn_k_lod1': _L0_attn_in['k_lod1'], 'L0_attn_v_lod1': _L0_attn_in['v_lod1'], 'L0_attn_k_lod2': _L0_attn_in['k_lod2'], 'L0_attn_v_lod2': _L0_attn_in['v_lod2'], 'L0_ffn_gate_weight': _L0_ffn_in['gate_weight'], 'L0_ffn_e_score_correction_bias': _L0_ffn_in['e_score_correction_bias'], 'L0_ffn_experts_gate_up': _L0_ffn_in['experts_gate_up'], 'L0_ffn_experts_down': _L0_ffn_in['experts_down'], 'L0_ffn_shared_gate_w': _L0_ffn_in['shared_gate_w'], 'L0_ffn_shared_up_w': _L0_ffn_in['shared_up_w'], 'L0_ffn_shared_down_w': _L0_ffn_in['shared_down_w']}
    _x0 = _d['L0_attn_x']
    _d['L0_attn_x'] = jax.random.normal(jax.random.fold_in(jax.random.key(seed), 1), (16, 512, 256), dtype=_x0.dtype)
    del _x0
    return _d

def reference(L0_attn_x, L0_attn_W_q, L0_attn_W_k, L0_attn_W_v, L0_attn_W_o, L0_attn_k_lod1, L0_attn_v_lod1, L0_attn_k_lod2, L0_attn_v_lod2, L0_ffn_gate_weight, L0_ffn_e_score_correction_bias, L0_ffn_experts_gate_up, L0_ffn_experts_down, L0_ffn_shared_gate_w, L0_ffn_shared_up_w, L0_ffn_shared_down_w):

    def _L0_attn_ref(x, W_q, W_k, W_v, W_o, k_lod1, v_lod1, k_lod2, v_lod2):
        import jax, jax.numpy as jnp
        import numpy as np
        B, S, D_MODEL = (1, 512, 256)
        H = 16
        D = D_MODEL // H
        G = 32
        TOP2, TOP1 = (4, 8)
        WIN = 128
        SCALE = D ** (-0.5)

        def _rotate_half(x):
            x1, x2 = jnp.split(x, 2, axis=-1)
            return jnp.concatenate([-x2, x1], axis=-1)

        def _rope(q, k):
            s = q.shape[2]
            inv_freq = 1.0 / 10000.0 ** (jnp.arange(0, D, 2, dtype=jnp.float32) / D)
            freqs = jnp.arange(s, dtype=jnp.float32)[:, None] * inv_freq[None, :]
            emb = jnp.concatenate([freqs, freqs], axis=-1)
            cos = jnp.cos(emb)[None, None]
            sin = jnp.sin(emb)[None, None]
            return (q * cos + _rotate_half(q) * sin, k * cos + _rotate_half(k) * sin)
        b, s, _ = x.shape
        q = (x @ W_q.T).reshape(b, s, H, D).transpose(0, 2, 1, 3)
        k = (x @ W_k.T).reshape(b, s, H, D).transpose(0, 2, 1, 3)
        v = (x @ W_v.T).reshape(b, s, H, D).transpose(0, 2, 1, 3)
        q, k = _rope(q, k)
        n1 = s // G
        k1 = k[:, :, :n1 * G].reshape(b, H, n1, G * D) @ k_lod1.T
        n2 = n1 // G
        if n2 > 0:
            k2 = k1[:, :, :n2 * G].reshape(b, H, n2, G * D) @ k_lod2.T
        else:
            k2 = k1
            n2 = n1
        scores2 = jnp.einsum('bhqd,bhkd->bhqk', q, k2) * SCALE
        q_pos = jnp.arange(s)
        lod2_end = jnp.arange(n2) * G * G + G * G - 1
        causal2 = lod2_end[None, :] < q_pos[:, None]
        scores2 = jnp.where(causal2[None, None], scores2, -jnp.inf)
        top2 = min(TOP2, n2)
        top2_idx = jax.lax.top_k(scores2, top2)[1]
        lod1_idx = jnp.clip(top2_idx[..., None] * G + jnp.arange(G), 0, n1 - 1)
        lod1_idx = lod1_idx.reshape(b, H, s, top2 * G)
        bi = jnp.arange(b)[:, None, None, None]
        hi = jnp.arange(H)[None, :, None, None]
        k1_g = k1[bi, hi, lod1_idx]
        scores1 = jnp.einsum('bhsd,bhstd->bhst', q, k1_g) * SCALE
        top1 = min(TOP1, scores1.shape[-1])
        top1_rel = jax.lax.top_k(scores1, top1)[1]
        top1_abs = jnp.take_along_axis(lod1_idx, top1_rel, axis=-1)
        pos = jnp.clip(top1_abs[..., None] * G + jnp.arange(G), 0, s - 1)
        pos = pos.reshape(b, H, s, top1 * G)
        si = jnp.arange(s)[None, None, :, None]
        attend = jnp.zeros((b, H, s, s), dtype=bool).at[bi, hi, si, pos].set(True)
        row = q_pos[:, None]
        col = q_pos[None, :]
        local = (col <= row) & (col >= row - WIN + 1)
        attend = (attend | local[None, None]) & (col <= row)[None, None]
        scores = jnp.einsum('bhqd,bhkd->bhqk', q, k) * SCALE
        scores = jnp.where(attend, scores, -jnp.inf)
        attn = jax.nn.softmax(scores, axis=-1)
        attn = jnp.where(jnp.isnan(attn), 0.0, attn)
        out = jnp.einsum('bhqk,bhkd->bhqd', attn, v)
        out = out.transpose(0, 2, 1, 3).reshape(b, s, D_MODEL)
        return out @ W_o.T

    def _L0_ffn_ref(x, gate_weight, e_score_correction_bias, experts_gate_up, experts_down, shared_gate_w, shared_up_w, shared_down_w):
        import jax, jax.numpy as jnp
        import numpy as np
        H = 256
        I = 128
        E = 32
        TOP_K = 6
        N_GROUP = 8
        TOPK_GROUP = 4
        SCALE = 2.5
        N_SHARED = 2
        SI = I * N_SHARED
        B, S = (2, 256)
        b, s, h = x.shape
        xf = x.reshape(-1, h)
        T = xf.shape[0]
        logits = xf.astype(jnp.float32) @ gate_weight.astype(jnp.float32).T
        scores = jax.nn.sigmoid(logits)
        sfc = scores + e_score_correction_bias[None, :]
        gs = E // N_GROUP
        group_scores = sfc.reshape(T, N_GROUP, gs).max(axis=-1)
        _, gidx = jax.lax.top_k(group_scores, TOPK_GROUP)
        gmask = jnp.zeros((T, N_GROUP), bool).at[jnp.arange(T)[:, None], gidx].set(True)
        smask = jnp.repeat(gmask, gs, axis=1)
        masked = jnp.where(smask, sfc, 0.0)
        _, topk_idx = jax.lax.top_k(masked, TOP_K)
        tw = jnp.take_along_axis(scores, topk_idx, axis=1)
        tw = tw / (tw.sum(-1, keepdims=True) + 1e-20)
        tw = (tw * SCALE).astype(xf.dtype)
        combine = jnp.zeros((T, E), xf.dtype).at[jnp.arange(T)[:, None], topk_idx].add(tw)

        def expert_step(acc, inp):
            gu, dn, c = inp
            g = xf @ gu[:I].T
            u = xf @ gu[I:].T
            o = jax.nn.silu(g) * u @ dn.T
            return (acc + c[:, None] * o, None)
        routed, _ = jax.lax.scan(expert_step, jnp.zeros_like(xf), (experts_gate_up, experts_down, combine.T))
        sh = jax.nn.silu(xf @ shared_gate_w.T) * (xf @ shared_up_w.T)
        shared_out = sh @ shared_down_w.T
        return (routed + shared_out).reshape(b, s, h)
    x = L0_attn_x
    xn = _layernorm(x, axis=-1)
    x = x + _L0_attn_ref(xn, L0_attn_W_q, L0_attn_W_k, L0_attn_W_v, L0_attn_W_o, L0_attn_k_lod1, L0_attn_v_lod1, L0_attn_k_lod2, L0_attn_v_lod2) + _L0_ffn_ref(xn, L0_ffn_gate_weight, L0_ffn_e_score_correction_bias, L0_ffn_experts_gate_up, L0_ffn_experts_down, L0_ffn_shared_gate_w, L0_ffn_shared_up_w, L0_ffn_shared_down_w)
    return x

_drawn_inputs = setup_inputs


def setup_inputs(seed=0):
    import zlib

    import numpy as np

    out = dict(_drawn_inputs(seed))
    spreads = {}
    factors = {'L0_attn_W_q': 8.0,
     'L0_attn_W_k': 8.0,
     'L0_attn_W_v': 4.433,
     'L0_attn_W_o': 4.525,
     'L0_attn_k_lod1': 8.0,
     'L0_ffn_gate_weight': 5.128,
     'L0_ffn_e_score_correction_bias': 8.0,
     'L0_ffn_experts_gate_up': 4.622,
     'L0_ffn_experts_down': 4.621,
     'L0_ffn_shared_gate_w': 3.384,
     'L0_ffn_shared_up_w': 3.347,
     'L0_ffn_shared_down_w': 3.348}
    for name, (base, spread) in spreads.items():
        noise = np.random.default_rng([zlib.crc32(name.encode()), seed]).standard_normal(out[name].shape)
        drawn = base * np.exp(spread * noise) if base else spread * noise
        out[name] = jnp.asarray(drawn.astype(out[name].dtype))
    for name, factor in factors.items():
        out[name] = (out[name] * factor).astype(out[name].dtype)
    return out
```

```python
from contextlib import ExitStack

import numpy as np

import concourse.bass as bass
from concourse import mybir

F32 = mybir.dt.float32
F32R = mybir.dt.float32r
BF16 = mybir.dt.bfloat16
I32 = mybir.dt.int32
U32 = mybir.dt.uint32
ALU = mybir.AluOpType
ACT = mybir.ActivationFunctionType
AX = mybir.AxisListType

P = 128
B, S, D = 16, 512, 256
T = B * S
NT = T // P
TB = S // P
KD = D // P
E, I = 32, 128
GROUPS, KEEP_GROUPS, TOPK = 8, 4, 6
ROUTE_SCALE = 2.5
SLOT_TILES = T * TOPK // P + E
BIG = 3.0e38
EPS = 1e-5


def front(nc, x, gate_wT, gate_bias, tri, ident, tok_iota, xn_d, xs_d, tab_d, K):
    ctx = ExitStack()
    with ctx:
        sb = lambda n, s, d: ctx.enter_context(nc.sbuf_tensor(n, s, d))
        ps = lambda n, s, d: ctx.enter_context(nc.psum_tensor(n, s, d))
        sem = lambda n: ctx.enter_context(nc.semaphore(n))

        xin = sb("xin", [P, NT, D], F32)
        xnorm = sb("xnorm", [P, 2, TB, D], F32)
        stats = sb("stats", [P, 4, 6], F32)
        meanvar = sb("meanvar", [P, NT, 2], F32)
        rstd = sb("rstd", [P, NT], F32)
        identf = sb("ident_front", [P, P], F32)
        tri_f = sb("tri_f", [P, 2 * P], F32)
        tri_b = sb("tri_b", [P, 2, P], BF16)
        gw = sb("gw", [P, KD, E], F32)
        gbias = sb("gbias", [P, E], F32)
        epst = sb("epst", [P, 1], F32)
        iota = sb("iota", [P, 5], F32)
        xT = sb("xT0", [P, 2, KD, S], F32)
        score = sb("score", [P, 2, TB, E], F32)
        sfc = sb("sfc", [P, TB, E], F32)
        gpad = sb("gpad", [P, TB, GROUPS + 4], F32)
        gtop = sb("gtop", [P, TB, 8], F32)
        grep = sb("grep", [P, TB, GROUPS + 4], F32)
        gsel = sb("gsel", [P, TB, GROUPS], F32)
        epad = sb("epad", [P, TB, E + 2], F32)
        etop = sb("etop", [P, TB, 8], F32)
        erep = sb("erep", [P, TB, E + 2], F32)
        sel = sb("sel", [P, TB, E], F32)
        wsel = sb("wsel", [P, TB, E], F32)
        wsum = sb("wsum", [P, TB], F32)
        comb = sb("comb", [P, NT, E], F32)
        selall = sb("selall", [P, NT, E], BF16)
        before = sb("before", [P, NT + 1, E], BF16)
        slot = sb("slot", [P, NT, E], F32)
        cnt = sb("cnt", [P, E], F32)
        cnti = sb("cnti", [P, E], I32)
        tiles = sb("tiles", [P, E], F32)
        acc = sb("acc", [P, 2, E], F32)
        base1 = sb("base1", [P, E], F32)
        padn = sb("padn", [P, 3, E], F32)
        tcmp = sb("tcmp", [P, 4, E], F32)
        ttab = sb("ttab", [P, 2, 4], F32)
        ttabi = sb("ttabi", [P, 2, 4], I32)
        top8 = sb("top8", [P, NT, 8], F32)
        eqw = sb("eqw", [P, TB, TOPK, E], F32)

        psT = ps("psT", [P, 2, S], F32)
        psL = ps("psL", [P, 2, S], F32)
        psR = ps("psR", [P, 2, S], F32)

        s_c = sem("consts_loaded")
        s_x = [sem(f"x_loaded{j}") for j in range(4)]
        s_v = sem("dve_step")
        s_vs = sem("dve_step_in_sequence")
        s_va = sem("dve_prep")
        s_st = sem("stats_done")
        s_sq = sem("sqrt_done")
        s_xn = sem("xn_ready")
        s_xst = [sem(f"xn_stored{c}") for c in range(2)]
        s_tr = sem("xT_in_psum")
        s_xt = sem("xT_ready")
        s_lg = sem("logits_ready")
        s_sc = sem("scores_ready")
        s_scu = sem("scores_used")
        s_sel = sem("selection_ready")
        s_rk = sem("ranks_ready")
        s_rkc = sem("ranks_copied")
        s_tot = sem("totals_ready")
        s_tt = sem("tile_tables_ready")
        s_td = sem("tile_tables_stored")

        x_v = x.rearrange("(g j) (t p) n -> g j p t n", j=4, p=P)
        xn_v = xn_d.rearrange("(b t p) n -> b p t n", t=TB, p=P)

        block = ctx.enter_context(nc.Block())

        @block.sync
        def _(sp):
            for j in range(4):
                sp.dma_start(xin[:, TB * j:TB * j + TB, :], x_v[0, j]).then_inc(s_x[j], 16)
                if j == 0:
                    sp.dma_start(tri_f[:], tri).then_inc(s_c, 16)
                    sp.dma_start(identf[:], ident).then_inc(s_c, 16)
                    sp.dma_start(gw[:], gate_wT.rearrange("(k p) e -> p k e", p=P)).then_inc(s_c, 16)
                    sp.dma_start(gbias[:], gate_bias.broadcast_to((P, E))).then_inc(s_c, 16)
                    sp.dma_start(iota[:], tok_iota).then_inc(s_c, 16)
            for g in range(1, B // 4):
                for j in range(4):
                    sp.wait_ge(s_x[j], 16 * g)
                    b = 4 * g + j
                    sp.dma_start(xin[:, TB * b:TB * b + TB, :], x_v[g, j]).then_inc(s_x[j], 16)
            with sp.Fori(0, B // 2) as h:
                for c in range(2):
                    b = 2 * h + c
                    sp.wait_ge(s_xn, b + 1)
                    sp.dma_start(xn_v[bass.ds(b, 1)].rearrange("o p t n -> p (o t) n"), xnorm[:, c]).then_inc(s_xst[c], 16)
            for c in range(2):
                sp.wait_ge(s_xst[c], 16 * B // 2)
            sp.wait_ge(s_tt, 1)
            sp.dma_start(tab_d.rearrange("w (c p) -> p w c", p=P), ttabi[:], allow_slow_non_contiguous=True).then_inc(s_td, 16)
            sp.wait_ge(s_td, 16)
            sp.dma_start(K.tables[0:1, :, :].rearrange("p w i -> p (w i)"), tab_d.rearrange("(o w) i -> o (w i)", o=1)).then_inc(s_td, 16)
            sp.wait_ge(s_td, 32)

        @block.scalar
        def _(act):
            act.wait_ge(s_st, 1)
            nc.scalar.activation(rstd[:], meanvar[:, :, 1], ACT.Sqrt, bias=epst[:, 0:1]).then_inc(s_sq, 1)
            with act.Fori(0, B // 2) as h:
                for c in range(2):
                    b = 2 * h + c
                    act.wait_ge(s_tr, b + 1)
                    if c == 1:
                        act.wait_ge(s_lg, b - 1)
                    else:
                        act.wait_ge(s_lg, b)
                    for k in range(KD):
                        ins = nc.scalar.copy(xT[:, c, k, :], psT[:, k, :])
                    ins.then_inc(s_xt, 1)
                    act.wait_ge(s_lg, b + 1)
                    if c == 0:
                        act.wait_ge(s_scu, b)
                    else:
                        act.wait_ge(s_scu, b - 1)
                    nc.scalar.activation(score[:, c], psL[:, c, 0:TB * E].rearrange("p (t e) -> p t e", t=TB),
                                         ACT.Sigmoid).then_inc(s_sc, 1)

        @block.tensor
        def _(pe):
            pe.wait_ge(s_c, 80)
            pe.wait_ge(s_va, 1)

            def transposes(b, c):
                pe.wait_ge(s_xn, b + 1)
                for k in range(KD):
                    for t in range(TB):
                        ins = nc.tensor.transpose(psT[:, k, P * t:P * t + P],
                                                  xnorm[:, c, t, P * k:P * k + P], identf[:])
                ins.then_inc(s_tr, 1)

            def logits(b, c):
                pe.wait_ge(s_xt, b + 1)
                if c == 0:
                    pe.wait_ge(s_sc, b)
                else:
                    pe.wait_ge(s_sc, b - 1)
                for t in range(TB):
                    for k in range(KD):
                        ins = nc.tensor.matmul(psL[:, c, E * t:E * t + E], xT[:, c, k, P * t:P * t + P], gw[:, k, :],
                                               start=(k == 0), stop=(k == KD - 1))
                ins.then_inc(s_lg, 1)

            def ranks(b, c):
                pe.wait_ge(s_sel, b + 1)
                if c == 0:
                    pe.wait_ge(s_rkc, b)
                else:
                    pe.wait_ge(s_rkc, b - 1)
                sl = selall[:, bass.ds(TB * b, TB), :].rearrange("p t e -> p (t e)")
                bf = before[:, bass.ds(TB * b, TB), :].rearrange("p t e -> p (t e)")
                nc.tensor.matmul(psR[:, c, 0:TB * E], tri_b[:, 0, :], sl, start=True, stop=False)
                nc.tensor.matmul(psR[:, c, 0:TB * E], tri_b[:, 1, :], bf, start=False, stop=True).then_inc(s_rk, 1)

            with pe.Fori(0, B // 2) as h:
                for c in range(2):
                    transposes(2 * h + c, c)
                    logits(2 * h + c, c)
                    ranks(2 * h + c, c)
            pe.wait_ge(s_rkc, B)
            nc.tensor.matmul(psR[:, 0, 0:E], tri_b[:, 1, :], before[:, NT, :], start=True, stop=True).then_inc(s_tot, 1)

        @block.vector
        def _(dve):
            n = [0]

            def prep(ins):
                n[0] += 1
                ins.then_inc(s_v, 1)
                dve.wait_ge(s_v, n[0])

            dve.wait_ge(s_c, 80)
            nc.vector.tensor_copy(tri_b[:].rearrange("p a b -> p (a b)"), tri_f[:]).then_inc(s_va, 1)
            nc.vector.memset(epst[:], EPS)
            nc.vector.memset(gpad[:], BIG)
            nc.vector.memset(epad[:], BIG)
            prep(nc.vector.memset(before[:], 0.0))
            for t in range(NT):
                b, j = t // TB, t % TB
                if j == 0:
                    dve.wait_ge(s_x[b % 4], 16 * (b // 4 + 1))
                prep(nc.vector.bn_stats(stats[:, j, :], xin[:, t, :]))
                ins = nc.vector.bn_aggr(meanvar[:, t, :], stats[:, j, :])
                if t == NT - 1:
                    ins.then_inc(s_st, 1)
            dve.wait_ge(s_sq, 1)
            prep(nc.vector.reciprocal(rstd[:], rstd[:]))

            def body(b, c, h):
                cnt_ = [0]

                def count(ins):
                    cnt_[0] += 1
                    ins.then_inc(s_vs, 1)

                def settle():
                    dve.wait_ge(s_vs, cnt_[0])

                def step(ins):
                    count(ins)
                    settle()

                dve.wait_ge(s_xst[c], 16 * h)
                if c == 0:
                    dve.wait_ge(s_tr, b)
                else:
                    dve.wait_ge(s_tr, b - 1)
                for t in range(TB):
                    tt = TB * b + t
                    xt_ = xin[:, bass.ds(tt, 1), :].rearrange("p o n -> p (o n)")
                    ins = nc.vector.tensor_scalar(
                        xnorm[:, c, t, :], xt_, meanvar[:, bass.ds(tt, 1), 0], rstd[:, bass.ds(tt, 1)],
                        ALU.subtract, ALU.mult)
                ins.then_inc(s_xn, 1)
                dve.wait_ge(s_sc, b + 1)
                step(nc.vector.tensor_tensor(sfc[:], score[:, c], gbias[:, None, :].broadcast_to((P, TB, E)), ALU.add))
                step(nc.vector.tensor_reduce(gpad[:, :, 0:GROUPS], sfc[:].rearrange("p t (g j) -> p t g j", g=GROUPS),
                                             AX.X, ALU.max))
                for t in range(TB):
                    count(nc.vector.max(gtop[:, t, :], gpad[:, t, :]))
                settle()
                for t in range(TB):
                    count(nc.vector.match_replace(grep[:, t, :], gtop[:, t, :], gpad[:, t, :], -BIG))
                settle()
                step(nc.vector.tensor_single_scalar(gsel[:], grep[:, :, 0:GROUPS], -BIG, ALU.is_equal))
                step(nc.vector.tensor_tensor(epad[:, :, 0:E].rearrange("p t (g j) -> p t g j", g=GROUPS),
                                             sfc[:].rearrange("p t (g j) -> p t g j", g=GROUPS),
                                             gsel[:, :, :, None].broadcast_to((P, TB, GROUPS, E // GROUPS)), ALU.mult))
                for t in range(TB):
                    count(nc.vector.max(etop[:, t, :], epad[:, t, :]))
                settle()
                for t in range(TB):
                    count(nc.vector.match_replace(erep[:, t, :], etop[:, t, :], epad[:, t, :], -BIG))
                settle()
                step(nc.vector.tensor_single_scalar(sel[:], erep[:, :, 0:E], -BIG, ALU.is_equal))
                step(nc.vector.tensor_copy(selall[:, bass.ds(TB * b, TB), :], sel[:]))
                step(nc.vector.tensor_tensor(wsel[:], score[:, c], sel[:], ALU.mult))
                step(nc.vector.tensor_reduce(wsum[:], wsel[:], AX.X, ALU.add))
                step(nc.vector.tensor_scalar(wsum[:], wsum[:], 1e-20, None, ALU.add))
                step(nc.vector.reciprocal(wsum[:], wsum[:]))
                nc.vector.scalar_tensor_tensor(comb[:, bass.ds(TB * b, TB), :], wsel[:], ROUTE_SCALE,
                                               wsum[:, :, None].broadcast_to((P, TB, E)),
                                               ALU.mult, ALU.mult).then_inc(s_scu, 1)
                for t in range(TB):
                    nx = before[:, bass.ds(TB * b + t + 1, 1), :].rearrange("p o e -> p (o e)")
                    pv = before[:, bass.ds(TB * b + t, 1), :].rearrange("p o e -> p (o e)")
                    ins = nc.vector.tensor_tensor(nx, pv, sel[:, t, :], ALU.add)
                    if t < TB - 1:
                        step(ins)
                ins.then_inc(s_sel, 1)
                dve.wait_ge(s_rk, b + 1)
                nc.vector.tensor_copy(slot[:, bass.ds(TB * b, TB), :].rearrange("p t e -> p (t e)"),
                                      psR[:, c, 0:TB * E]).then_inc(s_rkc, 1)
                dve.wait_ge(s_scu, b + 1)
                settle()
                dve.sem_inc(s_va, 1)
                dve.sem_clear(s_vs)

            with dve.Fori(0, B // 2) as h:
                for c in range(2):
                    body(2 * h + c, c, h)

            dve.wait_ge(s_tot, 1)
            prep(nc.vector.tensor_copy(cnt[:], psR[:, 0, 0:E]))
            prep(nc.vector.tensor_scalar(cnti[:], cnt[:], float(P - 1), None, ALU.add))
            prep(nc.vector.tensor_single_scalar(cnti[:], cnti[:], 7, ALU.arith_shift_right))
            prep(nc.vector.tensor_copy(tiles[:], cnti[:]))
            prep(nc.vector.tensor_copy(acc[:, 0, :], tiles[:]))
            a, sh = 0, 1
            while sh < E:
                nc.vector.tensor_copy(acc[:, 1 - a, 0:sh], acc[:, a, 0:sh])
                prep(nc.vector.tensor_tensor(acc[:, 1 - a, sh:E], acc[:, a, sh:E], acc[:, a, 0:E - sh], ALU.add))
                a, sh = 1 - a, 2 * sh
            ends = acc[:, a, :]
            prep(nc.vector.tensor_tensor(base1[:], ends, tiles[:], ALU.subtract))
            prep(nc.vector.tensor_scalar(base1[:], base1[:], float(P), 1.0, ALU.mult, ALU.add))
            prep(nc.vector.tensor_tensor(padn[:, 0, :], base1[:], cnt[:], ALU.add))
            prep(nc.vector.tensor_scalar(padn[:, 0, :], padn[:, 0, :], iota[:, 0:1], -1.0, ALU.add, ALU.add))
            prep(nc.vector.scalar_tensor_tensor(padn[:, 1, :], ends, float(P), padn[:, 0, :], ALU.mult, ALU.subtract))
            prep(nc.vector.tensor_scalar(padn[:, 1, :], padn[:, 1, :], 0.5, 1.0e6, ALU.is_lt, ALU.mult))
            prep(nc.vector.tensor_tensor(K.padslot[:], padn[:, 0, :], padn[:, 1, :], ALU.add))
            prep(nc.vector.tensor_tensor(tcmp[:], ends[:, None, :].broadcast_to((P, 4, E)),
                                         iota[:, 0:4, None].broadcast_to((P, 4, E)), ALU.is_le))
            prep(nc.vector.tensor_reduce(ttab[:, 0, :], tcmp[:], AX.X, ALU.add))
            prep(nc.vector.tensor_scalar(ttab[:, 0, :], ttab[:, 0, :], float(E - 1), None, ALU.min))
            prep(nc.vector.tensor_scalar(acc[:, 1 - a, 0:1], acc[:, a, E - 1:E], -1.0, None, ALU.add))
            prep(nc.vector.tensor_scalar(ttab[:, 1, :], iota[:, 0:4], acc[:, 1 - a, 0:1], None, ALU.min))
            nc.vector.tensor_copy(ttabi[:], ttab[:]).then_inc(s_tt, 1)
            prep(nc.vector.tensor_tensor(slot[:], slot[:], base1[:, None, :].broadcast_to((P, NT, E)), ALU.add))
            prep(nc.vector.tensor_tensor(slot[:], slot[:], selall[:], ALU.mult))
            for t in range(NT):
                ins = nc.vector.max(top8[:, t, :], slot[:, t, :])
            prep(ins)
            prep(nc.vector.tensor_scalar(K.slots[:], top8[:, :, 0:TOPK], -1.0, None, ALU.add))
            for b in range(B):
                tb = slice(TB * b, TB * b + TB)
                prep(nc.vector.tensor_tensor(eqw[:], slot[:, tb, None, :].broadcast_to((P, TB, TOPK, E)),
                                             top8[:, tb, 0:TOPK, None].broadcast_to((P, TB, TOPK, E)), ALU.is_equal))
                prep(nc.vector.tensor_tensor(eqw[:], eqw[:], comb[:, tb, None, :].broadcast_to((P, TB, TOPK, E)), ALU.mult))
                prep(nc.vector.tensor_reduce(K.weights[:, tb, :], eqw[:], AX.X, ALU.add))


def scatter_rows(nc, xn_d, xs_d, gate_upT, downT, K, W, ident, identf):
    R = 4
    ctx = ExitStack()
    with ctx:
        sb = lambda n, s, d: ctx.enter_context(nc.sbuf_tensor(n, s, d))
        sem = lambda n: ctx.enter_context(nc.semaphore(n))
        rows = sb("rows", [P, R, D], F32)
        zeros = sb("zeros", [P, D], F32)
        idx = sb("idx", [P, R, TOPK], U32)
        padi = sb("padi", [P, E], U32)
        s_w = sem("expert_weights_loaded")
        s_ld = [sem(f"rows_loaded{j}") for j in range(R)]
        s_ix = sem("slot_indices_copied")
        s_z = sem("zeros_ready")
        s_sc = [sem(f"rows_scattered{j}") for j in range(R)]
        s_pad = sem("padding_zeroed")
        s_pass = sem("wait_passed_scatter")
        xn_t = xn_d.rearrange("(t p) n -> t p n", p=P)
        block = ctx.enter_context(nc.Block())

        @block.scalar
        def _(act):
            act.dma_start(W.gate_up[:].rearrange("p e k n -> p (e k n)"), gate_upT.rearrange("p e k n -> p (e k n)")).then_inc(s_w, 16)
            act.dma_start(W.down[:].rearrange("p e n -> p (e n)"), downT.rearrange("p e n -> p (e n)")).then_inc(s_w, 16)
            act.dma_start(identf[:], ident).then_inc(s_w, 16)
            act.wait_ge(s_w, 48)

        @block.sync
        def _(sp):
            for j in range(R):
                sp.dma_start(rows[:, j, :], xn_t[j]).then_inc(s_ld[j], 16)
            with sp.Fori(1, NT // R) as g:
                for j in range(R):
                    sp.wait_ge(s_sc[j], 16 * TOPK * g)
                    sp.dma_start(rows[:, j, :], xn_t[bass.ds(R * g + j, 1)].rearrange("o p n -> (o p) n")).then_inc(s_ld[j], 16)

        @block.vector
        def _(dve):
            nc.vector.memset(zeros[:], 0.0).then_inc(s_z, 1)

        @block.gpsimd
        def _(pool):
            nc.gpsimd.tensor_copy(padi[:], K.padslot[:]).then_inc(s_ix, 1)
            pool.wait_ge(s_ix, 1)
            pool.wait_ge(s_z, 1)
            for e in range(E):
                nc.gpsimd.indirect_dma_start(xs_d, bass.IndirectOffsetOnAxis(ap=padi[:, e:e + 1], axis=0), zeros[:], None,
                                             bounds_check=SLOT_TILES * P - 1, oob_is_err=False).then_inc(s_pad, 16)
            with pool.Fori(0, NT // R) as g:
                for j in range(R):
                    pool.wait_ge(s_sc[j], 16 * TOPK * g)
                    nc.gpsimd.tensor_copy(idx[:, j, :], K.slots[:, bass.ds(R * g + j, 1), :].rearrange("p o k -> p (o k)")).then_inc(s_ix, 1)
                    pool.wait_ge(s_ix, R * g + j + 2)
                    pool.wait_ge(s_ld[j], 16 * g + 16)
                    pool.sem_inc(s_pass, 1)
                    for k in range(TOPK):
                        nc.gpsimd.indirect_dma_start(xs_d, bass.IndirectOffsetOnAxis(ap=idx[:, j, k:k + 1], axis=0),
                                                     rows[:, j, :], None).then_inc(s_sc[j], 16)
            for j in range(R):
                pool.wait_ge(s_sc[j], 16 * TOPK * (NT // R))
            pool.wait_ge(s_pad, 16 * E)


def experts(nc, xs_d, y_d, K, W, identf):
    R = 4
    ctx = ExitStack()
    with ctx:
        sb = lambda n, s, d: ctx.enter_context(nc.sbuf_tensor(n, s, d))
        ps = lambda n, s, d: ctx.enter_context(nc.psum_tensor(n, s, d))
        sem = lambda n: ctx.enter_context(nc.semaphore(n))
        xrow = sb("xrow", [P, R, D], F32)
        xT = sb("xT1", [P, 2, KD, P], F32)
        gate = sb("gate", [P, 2, I], F32)
        hid = sb("hid", [P, 2, I], F32)
        hT = sb("hT", [P, 2, P], F32)
        yrow = sb("yrow", [P, R, D], F32)
        psX = ps("psX", [P, 2, S], F32)
        psG = ps("psG", [P, 2, S], F32)
        psH = ps("psH", [P, 2, S], F32)
        psY = ps("psY", [P, 2, S], F32)
        s_xl = [sem(f"xrows_loaded{j}") for j in range(R)]
        s_ys = [sem(f"yrows_stored{j}") for j in range(R)]
        s_xtr = sem("x_transposed")
        s_xT = sem("xT_in_sbuf")
        s_gu = sem("gate_up_ready")
        s_g = sem("gate_silu_ready")
        s_h = sem("hidden_ready")
        s_htr = sem("hidden_transposed")
        s_hT = sem("hT_in_sbuf")
        s_y = sem("y_in_psum")
        s_yr = sem("y_in_sbuf")
        s_pass = sem("wait_passed_experts")
        xs_v = xs_d.rearrange("(t p) n -> t p n", p=P)
        y_v = y_d.rearrange("(t p) n -> t p n", p=P)
        N = SLOT_TILES
        assert N % R == 0
        block = ctx.enter_context(nc.Block())

        def turns(engine, turn):
            for s in range(0, 2 * R):
                turn(s, s // R, s % R, lambda d, s=s: s >= d)
            with engine.Fori(2, N // R) as g:
                for j in range(R):
                    turn(R * g + j, g, j, lambda d: True)
            for s in range(N, N + 4):
                turn(s, s // R, s % R, lambda d, s=s: s - d < N)

        def fills(g, j, back):
            return g + 1 if j >= back else g

        def later(t, n):
            return not isinstance(t, int) or t >= n

        @block.sync
        def _(sp):
            def turn(s, g, j, has):
                if has(0):
                    t = sp.value_load(K.tables[0:1, 1, bass.ds(s, 1)], min_val=0, max_val=N - 1)
                    if later(s, R):
                        sp.wait_ge(s_xtr, s - R + 1)
                        sp.sem_inc(s_pass, 1)
                    sp.dma_start(xrow[:, j, :], xs_v[bass.ds(t, 1)].rearrange("o p n -> (o p) n")).then_inc(s_xl[j], 16)
                if has(4):
                    y = s - 4
                    sp.wait_ge(s_yr, y + 1)
                    sp.dma_start(y_v[bass.ds(y, 1)].rearrange("o p n -> (o p) n"), yrow[:, j, :]).then_inc(s_ys[j], 16)
            turns(sp, turn)
            for j in range(R):
                sp.wait_ge(s_ys[j], 16 * (N // R))

        @block.tensor
        def _(pe):
            def turn(s, g, j, has):
                c = j % 2
                if has(0):
                    pe.wait_ge(s_xl[j], 16 * fills(g, j, 0))
                    if later(s, 2):
                        pe.wait_ge(s_xT, s - 1)
                    for k in range(KD):
                        ins = nc.tensor.transpose(psX[:, c, P * k:P * k + P], xrow[:, j, P * k:P * k + P], identf[:])
                    ins.then_inc(s_xtr, 1)
                if has(1):
                    t, d = s - 1, 1 - c
                    e = pe.value_load(K.tables[0:1, 0, bass.ds(t, 1)], min_val=0, max_val=E - 1)
                    pe.wait_ge(s_xT, t + 1)
                    if later(t, 2):
                        pe.wait_ge(s_h, t - 1)
                    for k in range(KD):
                        ins = nc.tensor.matmul(psG[:, d, 0:2 * I], xT[:, d, k, :],
                                               W.gate_up[:, bass.ds(e, 1), k, :].rearrange("p o n -> p (o n)"),
                                               start=(k == 0), stop=(k == KD - 1))
                    ins.then_inc(s_gu, 1)
                if has(2):
                    t, d = s - 2, c
                    pe.wait_ge(s_h, t + 1)
                    if later(t, 2):
                        pe.wait_ge(s_hT, t - 1)
                    nc.tensor.transpose(psH[:, d, 0:P], hid[:, d, :], identf[:]).then_inc(s_htr, 1)
                if has(3):
                    t, d = s - 3, 1 - c
                    e = pe.value_load(K.tables[0:1, 0, bass.ds(t, 1)], min_val=0, max_val=E - 1)
                    pe.wait_ge(s_hT, t + 1)
                    if later(t, 2):
                        pe.wait_ge(s_yr, t - 1)
                    nc.tensor.matmul(psY[:, d, 0:D], hT[:, d, :],
                                     W.down[:, bass.ds(e, 1), :].rearrange("p o n -> p (o n)"),
                                     start=True, stop=True).then_inc(s_y, 1)
            turns(pe, turn)

        @block.scalar
        def _(act):
            def turn(s, g, j, has):
                c = j % 2
                if has(1):
                    t, d = s - 1, 1 - c
                    act.wait_ge(s_gu, t + 1)
                    if later(t, 2):
                        act.wait_ge(s_h, t - 1)
                    nc.scalar.activation(gate[:, d, :], psG[:, d, 0:I], ACT.Silu).then_inc(s_g, 1)
                if has(2):
                    t, d = s - 2, c
                    act.wait_ge(s_htr, t + 1)
                    if later(t, 2):
                        act.wait_ge(s_y, t - 1)
                    nc.scalar.copy(hT[:, d, :], psH[:, d, 0:P]).then_inc(s_hT, 1)
            turns(act, turn)

        @block.vector
        def _(dve):
            def turn(s, g, j, has):
                c = j % 2
                if has(0):
                    dve.wait_ge(s_xtr, s + 1)
                    if later(s, 2):
                        dve.wait_ge(s_gu, s - 1)
                    nc.vector.tensor_copy(xT[:, c].rearrange("p k n -> p (k n)"), psX[:, c, 0:D]).then_inc(s_xT, 1)
                if has(1):
                    t, d = s - 1, 1 - c
                    dve.wait_ge(s_g, t + 1)
                    if later(t, 2):
                        dve.wait_ge(s_htr, t - 1)
                    nc.vector.tensor_tensor(hid[:, d, :], gate[:, d, :], psG[:, d, I:2 * I], ALU.mult).then_inc(s_h, 1)
                if has(3):
                    t, d, r = s - 3, 1 - c, (j - 3) % R
                    dve.wait_ge(s_y, t + 1)
                    if later(t, R):
                        dve.wait_ge(s_ys[r], 16 * (fills(g, j, 3) - 1))
                    nc.vector.tensor_copy(yrow[:, r, :], psY[:, d, 0:D]).then_inc(s_yr, 1)
            turns(dve, turn)


def combine(nc, part_d, y_d, out, K):
    R = 2
    ctx = ExitStack()
    with ctx:
        sb = lambda n, s, d: ctx.enter_context(nc.sbuf_tensor(n, s, d))
        sem = lambda n: ctx.enter_context(nc.semaphore(n))
        yk = sb("yk", [P, R, TOPK, D], F32)
        part = sb("part", [P, R, D], F32)
        idx = sb("idx2", [P, R, TOPK], U32)
        s_pl = [sem(f"part_loaded{j}") for j in range(R)]
        s_ix = sem("gather_indices_copied")
        s_gt = [sem(f"rows_gathered{j}") for j in range(R)]
        s_a = sem("sums_done")
        s_t = sem("tiles_summed")
        s_pass = sem("wait_passed_combine")
        s_o = [sem(f"out_stored{j}") for j in range(R)]
        part_v = part_d.rearrange("(t p) n -> t p n", p=P)
        out_v = out.rearrange("b (t p) n -> (b t) p n", p=P)
        block = ctx.enter_context(nc.Block())

        @block.sync
        def _(sp):
            for j in range(R):
                sp.dma_start(part[:, j, :], part_v[j]).then_inc(s_pl[j], 16)
            with sp.Fori(0, NT // R - 1) as g:
                for j in range(R):
                    t = R * g + j
                    sp.wait_ge(s_t, t + 1)
                    sp.dma_start(out_v[bass.ds(t, 1)].rearrange("o p n -> (o p) n"), part[:, j, :]).then_inc(s_o[j], 16)
                    sp.wait_ge(s_o[j], 16 * (g + 1))
                    sp.dma_start(part[:, j, :], part_v[bass.ds(t + R, 1)].rearrange("o p n -> (o p) n")).then_inc(s_pl[j], 16)
            for j in range(R):
                t = NT - R + j
                sp.wait_ge(s_t, t + 1)
                sp.dma_start(out_v[t], part[:, j, :]).then_inc(s_o[j], 16)
            for j in range(R):
                sp.wait_ge(s_o[j], 16 * (NT // R))

        @block.gpsimd
        def _(pool):
            with pool.Fori(0, NT // R) as g:
                for j in range(R):
                    t = R * g + j
                    pool.wait_ge(s_gt[j], 16 * TOPK * g)
                    nc.gpsimd.tensor_copy(idx[:, j, :], K.slots[:, bass.ds(t, 1), :].rearrange("p o k -> p (o k)")).then_inc(s_ix, 1)
                    pool.wait_ge(s_ix, t + 1)
                    pool.wait_ge(s_t, R * g)
                    pool.sem_inc(s_pass, 1)
                    for k in range(TOPK):
                        nc.gpsimd.indirect_dma_start(yk[:, j, k, :], None, y_d,
                                                     bass.IndirectOffsetOnAxis(ap=idx[:, j, k:k + 1], axis=0)).then_inc(s_gt[j], 16)

        @block.vector
        def _(dve):
            with dve.Fori(0, NT // R) as g:
                for j in range(R):
                    t = R * g + j
                    dve.wait_ge(s_pl[j], 16 * (g + 1))
                    dve.wait_ge(s_gt[j], 16 * TOPK * (g + 1))
                    for k in range(TOPK):
                        ins = nc.vector.scalar_tensor_tensor(part[:, j, :], yk[:, j, k, :],
                                                             K.weights[:, bass.ds(t, 1), k], part[:, j, :],
                                                             ALU.mult, ALU.add)
                        if k < TOPK - 1:
                            ins.then_inc(s_a, 1)
                            dve.wait_ge(s_a, (TOPK - 1) * t + k + 1)
                        else:
                            ins.then_inc(s_t, 1)



H, HD = 16, 16
HU = 8
NB = S // 32
NEG = -1.0e30
CAND = NB - 1 + 8
NCONST = 23


class Bank:

    def __init__(self, names, banks):
        self.bank = {x: i % banks for i, x in enumerate(names)}
        self.nth = {x: i // banks for i, x in enumerate(names)}
        self.uses = [sum(1 for i in range(len(names)) if i % banks == j) for j in range(banks)]

    def count(self, name, b):
        return self.uses[self.bank[name]] * b + self.nth[name] + 1


def attention(nc, x, xn_d, part_d, A, K):
    qs_d = nc.dram_tensor("q_split", (2, 2, HU, HD, S), F32).ap()
    ks_d = nc.dram_tensor("k_split", (2, 2, HU, HD, S), F32).ap()
    sel_d = nc.dram_tensor("sel_bias", (2, HU, NB, S - P), F32).ap()
    ctx = ExitStack()
    with ctx:
        sb = lambda n, s, d: ctx.enter_context(nc.sbuf_tensor(n, s, d))
        ps = lambda n, s, d: ctx.enter_context(nc.psum_tensor(n, s, d))
        sem = lambda n: ctx.enter_context(nc.semaphore(n))

        identf = sb("ident_attn", [P, P], F32)
        cb = sb("const_b", [P, 4, P], BF16)
        ident_b, part_b, caus_qk, caus_kq = (cb[:, i, :] for i in range(4))
        cos = sb("cos", [P, S], F32)
        sin = sb("sin", [P, S], F32)
        force = sb("force", [P, TB - 1, NB], F32)
        edge = sb("edge", [P, TB - 1, NB], F32)
        hmask = sb("hmask", [P, HU], F32)
        wq = sb("wq", [P, KD, D], F32)
        wk = sb("wk", [P, KD, D], F32)
        wv = sb("wv", [P, KD, D], F32)
        wo = sb("wo", [P, KD, D], F32)
        wsg = sb("wsg", [P, KD, D], F32)
        wsu = sb("wsu", [P, KD, D], F32)
        wsd = sb("wsd", [P, KD, D], F32)
        lod = sb("lod", [P, 32, P], F32)

        xnb = sb("xnb", [P, TB, D], F32)
        xT = sb("xTa", [P, KD, S], F32)
        vsb = sb("vsb", [P, TB, H, 32], F32)
        th = sb("th", [P, S], F32)
        shT = sb("shT", [P, KD, S], F32)
        r1 = sb("r1", [P, S], F32)
        r2 = sb("r2", [P, S], F32)
        qf = sb("qf", [P, S], F32)
        kf = sb("kf", [P, S], F32)
        split = sb("split", [P, 4, S], F32R)
        qst = [sb(f"qst{c}", [P, HU, S], F32R) for c in range(2)]
        kst = [sb(f"kst{c}", [P, HU, S], F32R) for c in range(2)]
        k1bd = sb("k1bd", [P, HU, CAND], F32)
        top8 = sb("top8a", [P, 3 * HU, 8], F32)
        rep = sb("rep", [P, 3 * HU, CAND], F32)
        bias = sb("bias", [P, 3 * HU, NB], F32)
        sbias = sb("sbias", [P, 3 * HU, NB], F32)
        spart = sb("spart", [P, 3 * HU], F32)
        selT = sb("selT", [P, 3 * P], F32R)
        diag = sb("diag", [P, 2, 3 * HU, P], BF16)
        m = sb("m", [P, HU, TB], F32)
        mT = sb("mT", [HU, 2, S], F32R)
        p0T = sb("p0T", [P, 2, 4, S], F32)
        p1T = sb("p1T", [P, 4, 3 * 2 * P], F32)
        oT = sb("oT", [P, S], F32)
        rs = sb("rs", [P, TB, 4], F32)
        on = sb("on", [P, TB, D], F32)
        oT2 = sb("oT2", [P, KD, S], F32)
        part = sb("part_a", [P, TB, D], F32)

        psA = ps("psA", [P, 2, S], F32)
        ps1 = ps("ps1", [P, 2, S], F32)
        ps2 = ps("ps2", [P, 2, S], F32)
        psO = ps("psO", [P, S], F32)
        psB = ps("psB", [P, S], F32)

        s_c = sem("a_consts_loaded")
        s_cv = sem("a_consts_ready")
        s_cz = sem("block_diagonal_cleared")
        s_pass = sem("wait_passed_attention")
        s_xb = sem("xn_loaded")
        s_xr = sem("residual_loaded")
        s_aR = [sem(f"a_bank_filled{j}") for j in range(2)]
        s_aF = [sem(f"a_bank_read{j}") for j in range(2)]
        s_1R = [sem(f"max_bank_filled{j}") for j in range(2)]
        s_1F = [sem(f"max_bank_read{j}") for j in range(2)]
        s_2R = [sem(f"exp_bank_filled{j}") for j in range(2)]
        s_2F = [sem(f"exp_bank_read{j}") for j in range(2)]
        s_bR = sem("b_bank_filled")
        s_bF = sem("b_bank_read")
        s_th = sem("tanh_ready")
        s_dv = sem("dve_step_a")
        s_q = sem("q_ready")
        s_k = sem("k_ready")
        s_wd = sem("split_stored")
        s_st = [sem(f"stack{c}_loaded") for c in range(2)]
        s_k1 = sem("k1_ready")
        s_sb = sem("sel_bias_ready")
        s_sp = sem("edge_bias_ready")
        s_sw = sem("selT_stored")
        s_sl = [sem(f"selT{c}_loaded") for c in range(2)]
        s_dg = sem("diag_ready")
        s_ml = [sem(f"max_rows{c}_loaded") for c in range(2)]
        s_pv = sem("pv_ready")
        s_oT = sem("oT_ready")
        s_ps = sem("part_stored")

        NA = ["xT0", "xT1", "V0", "V1", "G0", "U0", "G1", "U1"] + [f"{n}{c}" for c in range(2) for n in ("Q", "K", "k1_", "sa", "sb", "sT")]
        a = Bank(NA, 2)
        bb = Bank(["m0", "m1", "o0_0", "o1_0", "o0_1", "o1_1", "t0", "t1", "y0", "y1"], 1)
        PAIR = [((3,), (0,)), ((3,), (1,)), ((2, 0), (0,)), ((2, 0), (1,)), ((1,), (0, 1))]
        GROUP2 = [((0,), (h,)) for h in range(4)] + [((1, 3), (h,)) for h in range(4)] + [((2,), (0, 1)), ((2,), (2, 3))]
        IT1 = [(tiles, tuple(2 * p + h for h in hs)) for p in range(HU // 2) for tiles, hs in PAIR]
        IT2 = [(tiles, tuple(4 * g + h for h in hs)) for g in range(2) for tiles, hs in GROUP2]
        NI = len(IT1)
        PCOL = [0, 0, S, 3 * P]

        x_v = x.rearrange("b (t p) n -> b p t n", p=P)
        xn_v = xn_d.rearrange("(b t p) n -> b p t n", t=TB, p=P)
        part_v = part_d.rearrange("(b t p) n -> b p t n", t=TB, p=P)
        block = ctx.enter_context(nc.Block())

        @block.sync
        def _(sp):
            sp.wait_ge(s_cz, 1)
            loads = [(identf[:], A.ident), (r1[:].rearrange("p (i n) -> p i n", i=4), A.masks), (cos[:], A.cos), (sin[:], A.sin), (force[:], A.force),
                     (edge[:], A.edge), (hmask[:], A.hmask), (th[64:82, :], A.krows)]
            loads += [(dst[:], src.rearrange("(k p) n -> p k n", p=P)) for dst, src in
                      ((wq, A.WqT), (wk, A.WkT), (wv, A.WvT), (wo, A.WoT), (wsg, A.sgT), (wsu, A.suT), (wsd, A.sdT))]
            loads += [(lod[HD * h:HD * h + HD, :, HD * h:HD * h + HD], A.lod1) for h in range(HU)]
            assert len(loads) == NCONST
            for dst, src in loads:
                sp.dma_start(dst, src).then_inc(s_c, 16)
            with sp.Fori(0, B) as b:
                sp.wait_ge(s_aR[a.bank["xT1"]], a.uses[a.bank["xT1"]] * b)
                sp.dma_start(xnb[:], xn_v[bass.ds(b, 1)].rearrange("o p t n -> p (o t) n")).then_inc(s_xb, 16)
                sp.wait_ge(s_ps, 16 * b)
                sp.dma_start(part[:], x_v[bass.ds(b, 1)].rearrange("o p t n -> p (o t) n")).then_inc(s_xr, 16)
                for c in range(2):
                    u = 2 * b + c
                    for j, d in enumerate((qs_d, ks_d)):
                        sp.wait_ge((s_q, s_k)[j], u + 1)
                        for i in range(2):
                            sp.dma_start(d[c, i].rearrange("h d t -> (h d) t"), split[:, 2 * j + i, :].bitcast(F32)).then_inc(s_wd, 16)
                    sp.wait_ge(s_wd, 64 * u + 64)
                    sp.sem_inc(s_pass, 1)
                    sp.wait_ge(s_pv, 4 * b)
                    for r in range(4):
                        sp.dma_start(qst[c][HD * r:HD * r + HD].bitcast(F32), qs_d[c, r % 2].rearrange("h d t -> d h t")).then_inc(s_st[c], 16)
                        sp.dma_start(kst[c][HD * r:HD * r + HD].bitcast(F32), ks_d[c, r // 2].rearrange("h d t -> d h t")).then_inc(s_st[c], 16)
                    sp.wait_ge(s_aF[a.bank[f"sT{c}"]], a.count(f"sT{c}", b))
                    sp.dma_start(sel_d[c].rearrange("h j t -> (h j) t"), selT[:].bitcast(F32)).then_inc(s_sw, 16)
                    sp.wait_ge(s_sw, 16 * u + 16)
                    sp.dma_start(qst[c][64:80, :, P:S].bitcast(F32), sel_d[c].rearrange("h j t -> j h t")).then_inc(s_sl[c], 16)
                for c in range(2):
                    sp.wait_ge(s_bF, bb.count(f"m{c}", b))
                    for i in range(2):
                        sp.dma_start(qst[c][80 + i:81 + i, :, :].bitcast(F32), mT[:, i, :].bitcast(F32)).then_inc(s_ml[c], 16)
                sp.wait_ge(s_bF, bb.count("y1", b))
                sp.dma_start(part_v[bass.ds(b, 1)].rearrange("o p t n -> p (o t) n"), part[:]).then_inc(s_ps, 16)
            sp.wait_ge(s_ps, 16 * B)

        @block.tensor
        def _(pe):
            pe.wait_ge(s_c, 16 * NCONST)
            pe.wait_ge(s_cv, 1)

            def fill(name, b):
                j = a.bank[name]
                pe.wait_ge(s_aF[j], a.count(name, b) - 1)
                return psA[:, j, :], s_aR[j]

            def project(name, b, w, cols):
                o, ready = fill(name, b)
                for k in range(KD):
                    ins = nc.tensor.matmul(o, w[:, k, cols:cols + P], xT[:, k, :], start=(k == 0), stop=(k == KD - 1))
                ins.then_inc(ready, 1)

            def sequence_in(b):
                pe.wait_ge(s_xb, 16 * b + 16)
                for k in range(KD):
                    o, ready = fill(f"xT{k}", b)
                    for t in range(TB):
                        ins = nc.tensor.transpose(o[:, P * t:P * t + P], xnb[:, t, P * k:P * k + P], identf[:])
                    ins.then_inc(ready, 1)
                for k in range(KD):
                    pe.wait_ge(s_aF[a.bank[f"xT{k}"]], a.count(f"xT{k}", b))
                for v in range(2):
                    o, ready = fill(f"V{v}", b)
                    for t in range(2):
                        for k in range(KD):
                            ins = nc.tensor.matmul(o[:, D * t:D * t + D], xT[:, k, P * (2 * v + t):P * (2 * v + t) + P], wv[:, k, :],
                                                   start=(k == 0), stop=(k == KD - 1))
                    ins.then_inc(ready, 1)
                for i in range(2):
                    project(f"G{i}", b, wsg, P * i)
                    project(f"U{i}", b, wsu, P * i)

            def select(b, c):
                u = 2 * b + c
                project(f"Q{c}", b, wq, P * c)
                project(f"K{c}", b, wk, P * c)
                pe.wait_ge(s_k, u + 1)
                o, ready = fill(f"k1_{c}", b)
                for g in range(32):
                    ins = nc.tensor.matmul(o[:, 0:NB], lod[:, g, :], kf[:].rearrange("p (n g) -> p g n", g=32)[:, g, :],
                                           start=(g == 0), stop=(g == 31))
                ins.then_inc(ready, 1)
                pe.wait_ge(s_q, u + 1)
                pe.wait_ge(s_k1, u + 1)
                for name, tiles in (("sa", (1, 2)), ("sb", (3,))):
                    o, ready = fill(f"{name}{c}", b)
                    for i, t in enumerate(tiles):
                        ins = nc.tensor.matmul(o[:, i * HU * CAND:(i + 1) * HU * CAND], qf[:, P * t:P * t + P],
                                               k1bd[:].rearrange("p h j -> p (h j)"), start=True, stop=True)
                    ins.then_inc(ready, 1)
                pe.wait_ge(s_sb, u + 1)
                o, ready = fill(f"sT{c}", b)
                for t in range(3):
                    ins = nc.tensor.transpose(o[:, P * t:P * t + P],
                                              sbias[:, HU * t:HU * t + HU, :].rearrange("p h j -> p (h j)"), identf[:])
                ins.then_inc(ready, 1)

            def maxima(b, c):
                u = 2 * b + c
                pe.wait_ge(s_st[c], 128 * b + 128)
                pe.wait_ge(s_sl[c], 16 * b + 16)
                pe.wait_ge(s_dg, u + 1)
                for i, (tiles, heads) in enumerate(IT1):
                    j = i % 2
                    pe.wait_ge(s_1F[j], (NI // 2) * u + i // 2)
                    at = 0
                    for h in heads:
                        for t in tiles:
                            n = P * (t + 1)
                            nc.tensor.matmul(ps1[:, j, at:at + n], qst[c][0:80, h, P * t:P * t + P], kst[c][0:80, h, 0:n],
                                             start=True, stop=False)
                            if t > 0:
                                nc.tensor.matmul(ps1[:, j, at + n - 2 * P:at + n - P], diag[:, c, HU * (t - 1) + h, :], part_b,
                                                 start=False, stop=False)
                            ins = nc.tensor.matmul(ps1[:, j, at + n - P:at + n], ident_b, caus_qk, start=False, stop=True)
                            at += n
                    ins.then_inc(s_1R[j], 1)
                for j in range(2):
                    pe.wait_ge(s_1F[j], (NI // 2) * (u + 1))
                pe.wait_ge(s_bF, bb.count(f"m{c}", b) - 1)
                for t in range(TB):
                    ins = nc.tensor.transpose(psB[0:HU, P * t:P * t + P], m[:, :, t], identf[:])
                ins.then_inc(s_bR, 1)

            def probs(b, c):
                u = 2 * b + c
                pe.wait_ge(s_ml[c], 32 * b + 32)

                def scores(lo, hi):
                    for i in range(lo, hi):
                        tiles, heads = IT2[i]
                        j = i % 2
                        pe.wait_ge(s_2F[j], (NI // 2) * u + i // 2)
                        at = 0
                        for h in heads:
                            for t in tiles:
                                n = S - P * t
                                nc.tensor.matmul(ps2[:, j, at:at + n], kst[c][0:82, h, P * t:P * t + P], qst[c][0:82, h, P * t:S],
                                                 start=True, stop=False)
                                if t < TB - 1:
                                    nc.tensor.matmul(ps2[:, j, at + P:at + 2 * P], part_b, diag[:, c, HU * t + h, :],
                                                     start=False, stop=False)
                                ins = nc.tensor.matmul(ps2[:, j, at:at + P], ident_b, caus_kq, start=False, stop=True)
                                at += n
                        ins.then_inc(s_2R[j], 1)

                def times_v(g):
                    for j in range(2):
                        pe.wait_ge(s_2F[j], (NI // 2) * u + 5 * (g + 1))
                    if c == 0 and g == 0:
                        for v in range(2):
                            pe.wait_ge(s_aF[a.bank[f"V{v}"]], a.count(f"V{v}", b))
                    pe.wait_ge(s_oT, 2 * u + g)
                    for t in range(TB):
                        for hh in range(4):
                            p = p0T[:, g, hh, :] if t == 0 else p1T[:, hh, PCOL[t]:PCOL[t] + S - P * t]
                            ins = nc.tensor.matmul(psO[32 * hh:32 * hh + 32, P * t:S], vsb[:, t, HU * c + 4 * g + hh, :],
                                                   p, start=(t == 0), stop=(t == TB - 1), skip_group_check=True)
                    ins.then_inc(s_pv, 1)

                def to_rows(g):
                    pe.wait_ge(s_oT, 2 * u + g + 1)
                    pe.wait_ge(s_bF, bb.count(f"o{g}_{c}", b) - 1)
                    for t in range(TB):
                        ins = nc.tensor.transpose(psB[:, P * t:P * t + P], oT[:, P * t:P * t + P], identf[:])
                    ins.then_inc(s_bR, 1)

                scores(0, 14)
                times_v(0)
                scores(14, 20)
                to_rows(0)
                times_v(1)
                to_rows(1)

            def sequence_out(b):
                pe.wait_ge(s_bF, bb.count("o1_1", b))
                for k in range(KD):
                    pe.wait_ge(s_bF, bb.count(f"t{k}", b) - 1)
                    for t in range(TB):
                        ins = nc.tensor.transpose(psB[:, P * t:P * t + P], on[:, t, P * k:P * k + P], identf[:])
                    ins.then_inc(s_bR, 1)
                pe.wait_ge(s_bF, bb.count("t1", b))
                pe.wait_ge(s_aF[a.bank["G1"]], a.count("G1", b))
                for v in range(2):
                    pe.wait_ge(s_bF, bb.count(f"y{v}", b) - 1)
                    for t in range(2):
                        tok = P * (2 * v + t)
                        for k in range(KD):
                            nc.tensor.matmul(psB[:, D * t:D * t + D], oT2[:, k, tok:tok + P], wo[:, k, :], start=(k == 0), stop=False)
                        for k in range(KD):
                            ins = nc.tensor.matmul(psB[:, D * t:D * t + D], shT[:, k, tok:tok + P], wsd[:, k, :],
                                                   start=False, stop=(k == KD - 1))
                    ins.then_inc(s_bR, 1)

            with pe.Fori(0, B) as b:
                sequence_in(b)
                for c in range(2):
                    select(b, c)
                for c in range(2):
                    maxima(b, c)
                for c in range(2):
                    probs(b, c)
                sequence_out(b)

        @block.scalar
        def _(act):
            def filled(name, b):
                j = a.bank[name]
                act.wait_ge(s_aR[j], a.count(name, b))
                return psA[:, j, :], s_aF[j]

            def sequence_in(b):
                for j in range(2):
                    act.wait_ge(s_aR[j], a.uses[j] * b)
                for k in range(KD):
                    o, free = filled(f"xT{k}", b)
                    nc.scalar.copy(xT[:, k, :], o).then_inc(free, 1)
                act.wait_ge(s_pv, 4 * b)
                for v in range(2):
                    o, free = filled(f"V{v}", b)
                    for t in range(2):
                        ins = nc.scalar.copy(vsb[:, 2 * v + t, :, 0:HD],
                                             o[:, D * t:D * t + D].rearrange("p (h d) -> p h d", h=H))
                    ins.then_inc(free, 1)
                for i in range(2):
                    o, _ = filled(f"G{i}", b)
                    if i == 0:
                        act.wait_ge(s_aF[a.bank["U1"]], a.uses[a.bank["U1"]] * b)
                    else:
                        act.wait_ge(s_aF[a.bank["U0"]], a.count("U0", b))
                    nc.scalar.activation(th[:], o, ACT.Tanh, scale=0.5).then_inc(s_th, 1)

            def select(b, c):
                u = 2 * b + c
                o, free = filled(f"sT{c}", b)
                act.wait_ge(s_sw, 16 * u)
                nc.scalar.copy(selT[:], o[:, 0:3 * P]).then_inc(free, 1)
                act.wait_ge(s_sp, u + 1)
                act.wait_ge(s_pv, 4 * b)
                for i in range(3 * HU):
                    ins = nc.scalar.activation(diag[:, c, i, :], ident_b, ACT.Copy, scale=spart[:, i:i + 1])
                ins.then_inc(s_dg, 1)

            def copy_out(b, c, g):
                act.wait_ge(s_pv, 4 * b + 2 * c + g + 1)
                act.wait_ge(s_bR, bb.count(f"o{g}_{c}", b) - 1)
                nc.scalar.copy(oT[:], psO[:]).then_inc(s_oT, 1)

            def probs(b, c):
                u = 2 * b + c
                for i, (tiles, heads) in enumerate(IT2):
                    j, g = i % 2, i // 10
                    if i % 10 == 0 and (c, g) != (0, 0):
                        act.wait_ge(s_pv, 2 * u - 1 + g)
                    if i % 10 == 4:
                        act.wait_ge(s_pv, 2 * u + g)
                    act.wait_ge(s_2R[j], (NI // 2) * u + i // 2 + 1)
                    h0 = heads[0] % 4
                    if len(heads) == 1:
                        out, src = (p0T[:, g, h0, :] if tiles == (0,) else p1T[:, h0, 0:S]), ps2[:, j, :]
                    else:
                        out = p1T[:, h0:h0 + 2, PCOL[2]:PCOL[2] + 2 * P]
                        src = ps2[:, j, :].rearrange("p (h n) -> p h n", h=2)
                    nc.scalar.activation(out, src, ACT.Exp, scale=float(HD) ** -0.5).then_inc(s_2F[j], 1)
                    if i == 14:
                        copy_out(b, c, 0)
                copy_out(b, c, 1)

            def sequence_out(b):
                for k in range(KD):
                    act.wait_ge(s_bR, bb.count(f"t{k}", b))
                    nc.scalar.copy(oT2[:, k, :], psB[:]).then_inc(s_bF, 1)

            act.wait_ge(s_cv, 1)
            with act.Fori(0, B) as b:
                sequence_in(b)
                for c in range(2):
                    select(b, c)
                for c in range(2):
                    probs(b, c)
                sequence_out(b)

        @block.vector
        def _(dve):
            nc.vector.memset(lod[:], 0.0).then_inc(s_cz, 1)
            dve.wait_ge(s_c, 16 * NCONST)
            for c in range(2):
                nc.vector.memset(qst[c][64:80, :, 0:P].bitcast(F32), 0.0)
                for h in range(HU):
                    nc.vector.tensor_copy(kst[c][64:82, h, :], th[64:82, :])
            nc.vector.memset(vsb[:, :, :, HD:HD + 1], 1.0)
            nc.vector.memset(vsb[:, :, :, HD + 1:32], 0.0)
            nc.vector.tensor_copy(cb[:].rearrange("p i n -> p (i n)"), r1[:]).then_inc(s_cv, 1)
            dve.wait_ge(s_cv, 1)
            cnt_ = [0]

            def count(ins):
                cnt_[0] += 1
                ins.then_inc(s_dv, 1)

            def settle(b):
                dve.wait_ge(s_dv, cnt_[0])

            def step(b, ins):
                count(ins)
                settle(b)

            def filled(name, b):
                j = a.bank[name]
                dve.wait_ge(s_aR[j], a.count(name, b))
                return psA[:, j, :], s_aF[j]

            def read(name, b):
                dve.wait_ge(s_aF[a.bank[name]], a.count(name, b))

            def shared(b):
                for i in range(2):
                    o, free = filled(f"U{i}", b)
                    dve.wait_ge(s_th, 2 * b + i + 1)
                    nc.vector.scalar_tensor_tensor(r1[:], th[:], 1.0, o, ALU.add, ALU.mult).then_inc(free, 1)
                    read(f"U{i}", b)
                    o, free = filled(f"G{i}", b)
                    nc.vector.scalar_tensor_tensor(shT[:, i, :], r1[:], 0.5, o, ALU.mult, ALU.mult).then_inc(free, 1)
                    read(f"G{i}", b)

            def rotate(b, c, name, dst, n, ready):
                u = 2 * b + c
                o, free = filled(f"{name}{c}", b)
                step(b, nc.vector.tensor_tensor(r1[:], o, cos[:], ALU.mult))
                nc.vector.tensor_tensor(r2[:], o, sin[:], ALU.mult).then_inc(free, 1)
                read(f"{name}{c}", b)
                dve.sem_inc(s_pass, 1)
                step(b, nc.vector.stream_shuffle(r2[:], r2[:], [(i // HD) * HD + (i + HD // 2) % HD for i in range(32)]))
                step(b, nc.vector.tensor_tensor(dst[:], r1[:], r2[:], ALU.add))
                if n == 0:
                    dve.wait_ge(s_wd, 64 * u)
                step(b, nc.vector.tensor_copy(split[:, n, :], dst[:]))
                nc.vector.tensor_tensor(split[:, n + 1, :], dst[:], split[:, n, :], ALU.subtract).then_inc(ready, 1)

            def select(b, c):
                u = 2 * b + c
                rotate(b, c, "Q", qf, 0, s_q)
                rotate(b, c, "K", kf, 2, s_k)
                o, free = filled(f"k1_{c}", b)
                nc.vector.tensor_tensor(k1bd[:, :, 0:NB], o[:, None, 0:NB].broadcast_to((P, HU, NB)),
                                        hmask[:, :, None].broadcast_to((P, HU, NB)), ALU.mult).then_inc(free, 1)
                read(f"k1_{c}", b)
                nc.vector.tensor_copy(k1bd[:, :, NB:CAND], k1bd[:, :, NB - 1:NB].broadcast_to((P, HU, CAND - NB))).then_inc(s_k1, 1)
                for name, tiles in (("sa", (0, 1)), ("sb", (2,))):
                    o, free = filled(f"{name}{c}", b)
                    cand = o[:, 0:len(tiles) * HU * CAND].rearrange("p (i j) -> p i j", j=CAND)
                    i0, n = HU * tiles[0], HU * len(tiles)
                    dve.sem_inc(s_pass, 1)
                    for i in range(n):
                        count(nc.vector.max(top8[:, i0 + i, :], cand[:, i, :]))
                    settle(b)
                    for i in range(n):
                        ins = nc.vector.match_replace(rep[:, i0 + i, :], top8[:, i0 + i, :], cand[:, i, :], -BIG)
                        if i < n - 1:
                            count(ins)
                    ins.then_inc(free, 1)
                    settle(b)
                    read(f"{name}{c}", b)
                step(b, nc.vector.tensor_scalar(bias[:], rep[:, :, 0:NB], -BIG, -NEG, ALU.is_equal, ALU.mult))
                step(b, nc.vector.tensor_scalar(bias[:], bias[:], NEG, None, ALU.add))
                nc.vector.tensor_tensor(sbias[:].rearrange("p (t h) j -> p t h j", h=HU), bias[:].rearrange("p (t h) j -> p t h j", h=HU),
                                        force[:, :, None, :].broadcast_to((P, 3, HU, NB)), ALU.max).then_inc(s_sb, 1)
                step(b, nc.vector.tensor_tensor(bias[:].rearrange("p (t h) j -> p t h j", h=HU), bias[:].rearrange("p (t h) j -> p t h j", h=HU),
                                                edge[:, :, None, :].broadcast_to((P, 3, HU, NB)), ALU.mult))
                dve.wait_ge(s_dg, u)
                nc.vector.tensor_reduce(spart[:], bias[:], AX.X, ALU.add).then_inc(s_sp, 1)
                dve.wait_ge(s_sp, u + 1)

            def maxima(b, c):
                u = 2 * b + c
                for i, (tiles, heads) in enumerate(IT1):
                    j = i % 2
                    dve.wait_ge(s_1R[j], (NI // 2) * u + i // 2 + 1)
                    if len(heads) == 2:
                        ins = nc.vector.tensor_reduce(m[:, heads[0]:heads[0] + 2, 1], ps1[:, j, :].rearrange("p (h n) -> p h n", h=2),
                                                      AX.X, ALU.max)
                    else:
                        at = 0
                        for t in tiles:
                            n = P * (t + 1)
                            ins = nc.vector.tensor_reduce(m[:, heads[0], t:t + 1], ps1[:, j, at:at + n], AX.X, ALU.max)
                            at += n
                    ins.then_inc(s_1F[j], 1)
                dve.wait_ge(s_bR, bb.count(f"m{c}", b))
                if c == 0:
                    dve.wait_ge(s_ml[1], 32 * b)
                else:
                    dve.wait_ge(s_ml[0], 32 * b + 32)
                step(b, nc.vector.tensor_scalar(mT[:, 0, :], psB[0:HU, :], -1.0, None, ALU.mult))
                nc.vector.scalar_tensor_tensor(mT[:, 1, :], psB[0:HU, :], -1.0, mT[:, 0, :], ALU.mult, ALU.subtract).then_inc(s_bF, 1)

            def outputs(b, c):
                for g in range(2):
                    dve.wait_ge(s_bR, bb.count(f"o{g}_{c}", b))
                    o = psB[:].rearrange("p (t h d) -> p t h d", t=TB, h=4)
                    step(b, nc.vector.reciprocal(rs[:], o[:, :, :, HD]))
                    h0 = (HU * c + 4 * g) * HD
                    nc.vector.tensor_tensor(on[:, :, h0:h0 + 4 * HD].rearrange("p t (h d) -> p t h d", h=4), o[:, :, :, 0:HD],
                                            rs[:, :, :, None].broadcast_to((P, TB, 4, HD)), ALU.mult).then_inc(s_bF, 1)
                    dve.wait_ge(s_bF, bb.count(f"o{g}_{c}", b))

            def sequence_out(b):
                dve.wait_ge(s_xr, 16 * b + 16)
                for v in range(2):
                    dve.wait_ge(s_bR, bb.count(f"y{v}", b))
                    nc.vector.tensor_tensor(part[:, 2 * v:2 * v + 2, :].rearrange("p t n -> p (t n)"),
                                            part[:, 2 * v:2 * v + 2, :].rearrange("p t n -> p (t n)"), psB[:], ALU.add).then_inc(s_bF, 1)

            with dve.Fori(0, B) as b:
                shared(b)
                for c in range(2):
                    select(b, c)
                for c in range(2):
                    maxima(b, c)
                for c in range(2):
                    outputs(b, c)
                sequence_out(b)
                settle(b)
                dve.sem_inc(s_pass, 1)
                dve.sem_clear(s_dv)


class Kept:
    pass


def program(nc, ins, out):
    xn_d = nc.dram_tensor("xn_d", (T, D), F32).ap()
    xs_d = nc.dram_tensor("xs_d", (SLOT_TILES * P, D), F32).ap()
    y_d = nc.dram_tensor("y_d", (SLOT_TILES * P, D), F32).ap()
    part_d = nc.dram_tensor("part_d", (T, D), F32).ap()
    tab_d = nc.dram_tensor("tab_d", (2, 4 * P), I32).ap()
    K, W, A = Kept(), Kept(), Kept()
    A.ident, A.masks, A.cos, A.sin, A.force, A.edge, A.hmask, A.krows = (
        ins[n] for n in ("ident", "masks", "cos", "sin", "force", "edge", "hmask", "krows"))
    A.WqT, A.WkT, A.WvT, A.WoT, A.sgT, A.suT, A.sdT, A.lod1 = (
        ins[n] for n in ("WqT", "WkT", "WvT", "WoT", "sgT", "suT", "sdT", "lod1"))
    with ExitStack() as ctx:
        sb = lambda n, s, d: ctx.enter_context(nc.sbuf_tensor(n, s, d))
        K.slots = sb("slots", [P, NT, TOPK], U32)
        K.weights = sb("weights", [P, NT, TOPK], F32)
        tctx = ctx.enter_context(ExitStack())
        K.padslot = tctx.enter_context(nc.sbuf_tensor("padslot", [P, E], U32))
        K.tables = tctx.enter_context(nc.sbuf_tensor("tables", [P, 2, 4 * P], I32))
        front(nc, ins["x"], ins["gate_wT"], ins["gate_bias"], ins["tri"], ins["ident"], ins["tok_iota"], xn_d, xs_d, tab_d, K)
        with ExitStack() as wctx:
            wsb = lambda n, s, d: wctx.enter_context(nc.sbuf_tensor(n, s, d))
            identf = wsb("identf", [P, P], F32)
            W.gate_up = wsb("w_gate_up", [P, E, KD, 2 * I], F32)
            W.down = wsb("w_down", [P, E, D], F32)
            scatter_rows(nc, xn_d, xs_d, ins["gate_upT"], ins["downT"], K, W, ins["ident"], identf)
            experts(nc, xs_d, y_d, K, W, identf)
        tctx.close()
        attention(nc, ins["x"], xn_d, part_d, A, K)
        combine(nc, part_d, y_d, out, K)


def laid_out(inputs):
    a = {k: np.ascontiguousarray(np.asarray(v)) for k, v in inputs.items()}
    c = np.ascontiguousarray
    one = np.ones((P, P), np.float32)
    r = np.arange(P)
    key, qry = r[None, :], r[:, None]
    inv = (1.0 / np.float32(10000.0) ** (np.arange(0, HD, 2, dtype=np.float32) / np.float32(HD))).astype(np.float32)
    ang = np.arange(S, dtype=np.float32)[None, :] * inv[r % (HD // 2)][:, None]
    sign = np.where(r % HD < HD // 2, 1.0, -1.0).astype(np.float32)[:, None]
    blk = (P * np.arange(1, TB)[None, :] + r[:, None]) // 32
    j = np.arange(NB)[None, None, :]
    eye = np.eye(P, dtype=np.float32)
    edge_keys = ((qry // 32 == key // 32) & (key % 32 <= qry % 32)).astype(np.float32)
    later = np.where(key > qry, np.float32(NEG), np.float32(0.0)).astype(np.float32)
    return {
        "x": a["L0_attn_x"],
        "gate_wT": c(a["L0_ffn_gate_weight"].T),
        "gate_bias": a["L0_ffn_e_score_correction_bias"].reshape(1, E),
        "gate_upT": c(a["L0_ffn_experts_gate_up"].reshape(E, 2 * I, KD, P).transpose(3, 0, 2, 1)),
        "downT": c(a["L0_ffn_experts_down"].transpose(2, 0, 1)),
        "tri": np.concatenate([np.triu(one, 1), one], axis=1),
        "ident": eye,
        "tok_iota": c((r.astype(np.float32)[:, None] + P * np.arange(5, dtype=np.float32)[None, :])),
        "WqT": c(a["L0_attn_W_q"].T), "WkT": c(a["L0_attn_W_k"].T), "WvT": c(a["L0_attn_W_v"].T), "WoT": c(a["L0_attn_W_o"].T),
        "sgT": c(a["L0_ffn_shared_gate_w"].T), "suT": c(a["L0_ffn_shared_up_w"].T), "sdT": c(a["L0_ffn_shared_down_w"].T),
        "lod1": c(a["L0_attn_k_lod1"].reshape(HD, 32, HD).transpose(2, 1, 0)),
        "masks": c(np.stack([eye, edge_keys, later, later.T], axis=1)),
        "cos": np.cos(ang), "sin": np.sin(ang) * sign,
        "force": c(np.where(j >= blk[:, :, None] - 4, np.float32(0.0), np.float32(NEG)).astype(np.float32)),
        "edge": c((j == blk[:, :, None] - 4).astype(np.float32)),
        "hmask": c((r[:, None] // HD == np.arange(HU)[None, :]).astype(np.float32)),
        "krows": c(np.concatenate([(np.arange(S)[None, :] // 32 == np.arange(NB)[:, None]).astype(np.float32),
                                   np.ones((2, S), np.float32)])),
    }


def kernel(**inputs):
    import concourse.bacc as _bacc
    from concourse.bass_utils import run_bass_kernel_spmd as _run

    nc = _bacc.Bacc("TRN2", target_bir_lowering=False, num_devices=1)
    arrays, args = {}, {}
    for name, a in laid_out(inputs).items():
        arrays[f"in_{name}"] = a
        args[name] = nc.dram_tensor(f"in_{name}", a.shape, mybir.dt.from_np(a.dtype), kind="ExternalInput").ap()
    out = nc.dram_tensor("out_0", (B, S, D), F32, kind="ExternalOutput").ap()
    program(nc, args, out)
    r = _run(nc, [arrays], core_ids=[0])
    return r.results[0]["out_0"]
```

```python
from contextlib import ExitStack

import numpy as np

import concourse.bass as bass
from concourse import mybir

F32 = mybir.dt.float32
F32R = mybir.dt.float32r
BF16 = mybir.dt.bfloat16
I32 = mybir.dt.int32
U32 = mybir.dt.uint32
ALU = mybir.AluOpType
ACT = mybir.ActivationFunctionType
AX = mybir.AxisListType

P = 128
B, S, D = 16, 512, 256
T = B * S
NT = T // P
TB = S // P
KD = D // P
E, I = 32, 128
GROUPS, KEEP_GROUPS, TOPK = 8, 4, 6
ROUTE_SCALE = 2.5
SLOT_TILES = T * TOPK // P + E
BIG = 3.0e38
EPS = 1e-5


def front(nc, x, gate_wT, gate_bias, tri, ident, tok_iota, xn_d, xs_d, tab_d, K):
    ctx = ExitStack()
    with ctx:
        sb = lambda n, s, d: ctx.enter_context(nc.sbuf_tensor(n, s, d))
        ps = lambda n, s, d: ctx.enter_context(nc.psum_tensor(n, s, d))
        sem = lambda n: ctx.enter_context(nc.semaphore(n))

        xin = sb("xin", [P, NT, D], F32)
        xnorm = sb("xnorm", [P, 2, TB, D], F32)
        stats = sb("stats", [P, 4, 6], F32)
        meanvar = sb("meanvar", [P, NT, 2], F32)
        rstd = sb("rstd", [P, NT], F32)
        identf = sb("ident_front", [P, P], F32)
        tri_f = sb("tri_f", [P, 2 * P], F32)
        tri_b = sb("tri_b", [P, 2, P], BF16)
        gw = sb("gw", [P, KD, E], F32)
        gbias = sb("gbias", [P, E], F32)
        epst = sb("epst", [P, 1], F32)
        iota = sb("iota", [P, 5], F32)
        xT = sb("xT0", [P, 2, KD, S], F32)
        score = sb("score", [P, 2, TB, E], F32)
        sfc = sb("sfc", [P, TB, E], F32)
        gpad = sb("gpad", [P, TB, GROUPS + 4], F32)
        gtop = sb("gtop", [P, TB, 8], F32)
        grep = sb("grep", [P, TB, GROUPS + 4], F32)
        gsel = sb("gsel", [P, TB, GROUPS], F32)
        epad = sb("epad", [P, TB, E + 2], F32)
        etop = sb("etop", [P, TB, 8], F32)
        erep = sb("erep", [P, TB, E + 2], F32)
        sel = sb("sel", [P, TB, E], F32)
        wsel = sb("wsel", [P, TB, E], F32)
        wsum = sb("wsum", [P, TB], F32)
        comb = sb("comb", [P, NT, E], F32)
        selall = sb("selall", [P, NT, E], BF16)
        before = sb("before", [P, NT + 1, E], BF16)
        slot = sb("slot", [P, NT, E], F32)
        cnt = sb("cnt", [P, E], F32)
        cnti = sb("cnti", [P, E], I32)
        tiles = sb("tiles", [P, E], F32)
        acc = sb("acc", [P, 2, E], F32)
        base1 = sb("base1", [P, E], F32)
        padn = sb("padn", [P, 3, E], F32)
        tcmp = sb("tcmp", [P, 4, E], F32)
        ttab = sb("ttab", [P, 2, 4], F32)
        ttabi = sb("ttabi", [P, 2, 4], I32)
        top8 = sb("top8", [P, NT, 8], F32)
        eqw = sb("eqw", [P, TB, TOPK, E], F32)

        psT = ps("psT", [P, 2, S], F32)
        psL = ps("psL", [P, 2, S], F32)
        psR = ps("psR", [P, 2, S], F32)

        s_c = sem("consts_loaded")
        s_x = [sem(f"x_loaded{j}") for j in range(4)]
        s_v = sem("dve_step")
        s_vs = sem("dve_step_in_sequence")
        s_va = sem("dve_prep")
        s_st = sem("stats_done")
        s_sq = sem("sqrt_done")
        s_xn = sem("xn_ready")
        s_xst = [sem(f"xn_stored{c}") for c in range(2)]
        s_tr = sem("xT_in_psum")
        s_xt = sem("xT_ready")
        s_lg = sem("logits_ready")
        s_sc = sem("scores_ready")
        s_scu = sem("scores_used")
        s_sel = sem("selection_ready")
        s_rk = sem("ranks_ready")
        s_rkc = sem("ranks_copied")
        s_tot = sem("totals_ready")
        s_tt = sem("tile_tables_ready")
        s_td = sem("tile_tables_stored")

        x_v = x.rearrange("(g j) (t p) n -> g j p t n", j=4, p=P)
        xn_v = xn_d.rearrange("(b t p) n -> b p t n", t=TB, p=P)

        block = ctx.enter_context(nc.Block())

        @block.sync
        def _(sp):
            for j in range(4):
                sp.dma_start(xin[:, TB * j:TB * j + TB, :], x_v[0, j]).then_inc(s_x[j], 16)
                if j == 0:
                    sp.dma_start(tri_f[:], tri).then_inc(s_c, 16)
                    sp.dma_start(identf[:], ident).then_inc(s_c, 16)
                    sp.dma_start(gw[:], gate_wT.rearrange("(k p) e -> p k e", p=P)).then_inc(s_c, 16)
                    sp.dma_start(gbias[:], gate_bias.broadcast_to((P, E))).then_inc(s_c, 16)
                    sp.dma_start(iota[:], tok_iota).then_inc(s_c, 16)
            for g in range(1, B // 4):
                for j in range(4):
                    sp.wait_ge(s_x[j], 16 * g)
                    b = 4 * g + j
                    sp.dma_start(xin[:, TB * b:TB * b + TB, :], x_v[g, j]).then_inc(s_x[j], 16)
            with sp.Fori(0, B // 2) as h:
                for c in range(2):
                    b = 2 * h + c
                    sp.wait_ge(s_xn, b + 1)
                    sp.dma_start(xn_v[bass.ds(b, 1)].rearrange("o p t n -> p (o t) n"), xnorm[:, c]).then_inc(s_xst[c], 16)
            for c in range(2):
                sp.wait_ge(s_xst[c], 16 * B // 2)
            sp.wait_ge(s_tt, 1)
            sp.dma_start(tab_d.rearrange("w (c p) -> p w c", p=P), ttabi[:], allow_slow_non_contiguous=True).then_inc(s_td, 16)
            sp.wait_ge(s_td, 16)

        @block.scalar
        def _(act):
            act.wait_ge(s_st, 1)
            nc.scalar.activation(rstd[:], meanvar[:, :, 1], ACT.Sqrt, bias=epst[:, 0:1]).then_inc(s_sq, 1)
            def body(h):
                for c in range(2):
                    b = 2 * h + c
                    act.wait_ge(s_tr, b + 1)
                    act.wait_ge(s_lg, 2 * h)
                    for k in range(KD):
                        ins = nc.scalar.copy(xT[:, c, k, :], psT[:, k, :])
                    ins.then_inc(s_xt, 1)
                    act.wait_ge(s_lg, b + 1)
                    if not isinstance(h, int) or h > 0:
                        act.wait_ge(s_scu, b - 1)
                    nc.scalar.activation(score[:, c], psL[:, c, 0:TB * E].rearrange("p (t e) -> p t e", t=TB),
                                         ACT.Sigmoid).then_inc(s_sc, 1)

            body(0)
            with act.Fori(1, B // 2) as h:
                body(h)

        @block.tensor
        def _(pe):
            pe.wait_ge(s_c, 80)
            pe.wait_ge(s_va, 1)

            def transposes(b, c):
                pe.wait_ge(s_xn, b + 1)
                for k in range(KD):
                    for t in range(TB):
                        ins = nc.tensor.transpose(psT[:, k, P * t:P * t + P],
                                                  xnorm[:, c, t, P * k:P * k + P], identf[:])
                ins.then_inc(s_tr, 1)

            def logits(b, c):
                pe.wait_ge(s_xt, b + 1)
                pe.wait_ge(s_sc, b - c)
                for t in range(TB):
                    for k in range(KD):
                        ins = nc.tensor.matmul(psL[:, c, E * t:E * t + E], xT[:, c, k, P * t:P * t + P], gw[:, k, :],
                                               start=(k == 0), stop=(k == KD - 1))
                ins.then_inc(s_lg, 1)

            def ranks(b, c):
                pe.wait_ge(s_sel, b + 1)
                pe.wait_ge(s_rkc, b - c)
                sl = selall[:, bass.ds(TB * b, TB), :].rearrange("p t e -> p (t e)")
                bf = before[:, bass.ds(TB * b, TB), :].rearrange("p t e -> p (t e)")
                nc.tensor.matmul(psR[:, c, 0:TB * E], tri_b[:, 0, :], sl, start=True, stop=False)
                nc.tensor.matmul(psR[:, c, 0:TB * E], tri_b[:, 1, :], bf, start=False, stop=True).then_inc(s_rk, 1)

            def body(h, last=False):
                for c in range(2):
                    if not (last and c == 1):
                        transposes(2 * h + c + 1, 1 - c)
                        logits(2 * h + c + 1, 1 - c)
                    ranks(2 * h + c, c)

            transposes(0, 0)
            logits(0, 0)
            body(0)
            with pe.Fori(1, B // 2 - 1) as h:
                body(h)
            body(B // 2 - 1, last=True)
            pe.wait_ge(s_rkc, B)
            nc.tensor.matmul(psR[:, 0, 0:E], tri_b[:, 1, :], before[:, NT, :], start=True, stop=True).then_inc(s_tot, 1)

        @block.vector
        def _(dve):
            n = [0]

            def prep(ins):
                n[0] += 1
                ins.then_inc(s_v, 1)
                dve.wait_ge(s_v, n[0])

            dve.wait_ge(s_c, 80)
            nc.vector.tensor_copy(tri_b[:].rearrange("p a b -> p (a b)"), tri_f[:]).then_inc(s_va, 1)
            nc.vector.memset(epst[:], EPS)
            nc.vector.memset(gpad[:], BIG)
            nc.vector.memset(epad[:], BIG)
            prep(nc.vector.memset(before[:], 0.0))
            for t in range(NT):
                b, j = t // TB, t % TB
                if j == 0:
                    dve.wait_ge(s_x[b % 4], 16 * (b // 4 + 1))
                prep(nc.vector.bn_stats(stats[:, j, :], xin[:, t, :]))
                ins = nc.vector.bn_aggr(meanvar[:, t, :], stats[:, j, :])
                if t == NT - 1:
                    ins.then_inc(s_st, 1)
            dve.wait_ge(s_sq, 1)
            prep(nc.vector.reciprocal(rstd[:], rstd[:]))

            def normalise(b, c, h):
                dve.wait_ge(s_xst[c], 16 * h)
                dve.wait_ge(s_tr, b - c)
                for t in range(TB):
                    tt = TB * b + t
                    xt_ = xin[:, bass.ds(tt, 1), :].rearrange("p o n -> p (o n)")
                    ins = nc.vector.tensor_scalar(
                        xnorm[:, c, t, :], xt_, meanvar[:, bass.ds(tt, 1), 0], rstd[:, bass.ds(tt, 1)],
                        ALU.subtract, ALU.mult)
                ins.then_inc(s_xn, 1)

            def route(b, c):
                cnt_ = [0]

                def count(ins):
                    cnt_[0] += 1
                    ins.then_inc(s_vs, 1)

                def settle():
                    dve.wait_ge(s_vs, cnt_[0])

                def step(ins):
                    count(ins)
                    settle()

                dve.wait_ge(s_sc, b + 1)
                step(nc.vector.tensor_tensor(sfc[:], score[:, c], gbias[:, None, :].broadcast_to((P, TB, E)), ALU.add))
                step(nc.vector.tensor_reduce(gpad[:, :, 0:GROUPS], sfc[:].rearrange("p t (g j) -> p t g j", g=GROUPS),
                                             AX.X, ALU.max))
                for t in range(TB):
                    count(nc.vector.max(gtop[:, t, :], gpad[:, t, :]))
                settle()
                for t in range(TB):
                    count(nc.vector.match_replace(grep[:, t, :], gtop[:, t, :], gpad[:, t, :], -BIG))
                settle()
                step(nc.vector.tensor_single_scalar(gsel[:], grep[:, :, 0:GROUPS], -BIG, ALU.is_equal))
                step(nc.vector.tensor_tensor(epad[:, :, 0:E].rearrange("p t (g j) -> p t g j", g=GROUPS),
                                             sfc[:].rearrange("p t (g j) -> p t g j", g=GROUPS),
                                             gsel[:, :, :, None].broadcast_to((P, TB, GROUPS, E // GROUPS)), ALU.mult))
                for t in range(TB):
                    count(nc.vector.max(etop[:, t, :], epad[:, t, :]))
                settle()
                for t in range(TB):
                    count(nc.vector.match_replace(erep[:, t, :], etop[:, t, :], epad[:, t, :], -BIG))
                settle()
                step(nc.vector.tensor_single_scalar(sel[:], erep[:, :, 0:E], -BIG, ALU.is_equal))
                step(nc.vector.tensor_copy(selall[:, bass.ds(TB * b, TB), :], sel[:]))
                step(nc.vector.tensor_tensor(wsel[:], score[:, c], sel[:], ALU.mult))
                step(nc.vector.tensor_reduce(wsum[:], wsel[:], AX.X, ALU.add))
                step(nc.vector.tensor_scalar(wsum[:], wsum[:], 1e-20, None, ALU.add))
                step(nc.vector.reciprocal(wsum[:], wsum[:]))
                nc.vector.scalar_tensor_tensor(comb[:, bass.ds(TB * b, TB), :], wsel[:], ROUTE_SCALE,
                                               wsum[:, :, None].broadcast_to((P, TB, E)),
                                               ALU.mult, ALU.mult).then_inc(s_scu, 1)
                for t in range(TB):
                    nx = before[:, bass.ds(TB * b + t + 1, 1), :].rearrange("p o e -> p (o e)")
                    pv = before[:, bass.ds(TB * b + t, 1), :].rearrange("p o e -> p (o e)")
                    ins = nc.vector.tensor_tensor(nx, pv, sel[:, t, :], ALU.add)
                    if t < TB - 1:
                        step(ins)
                ins.then_inc(s_sel, 1)
                dve.wait_ge(s_rk, b + 1)
                nc.vector.tensor_copy(slot[:, bass.ds(TB * b, TB), :].rearrange("p t e -> p (t e)"),
                                      psR[:, c, 0:TB * E]).then_inc(s_rkc, 1)
                dve.wait_ge(s_scu, b + 1)
                settle()
                dve.sem_inc(s_va, 1)
                dve.sem_clear(s_vs)

            def body(h, last=False):
                for c in range(2):
                    if not (last and c == 1):
                        normalise(2 * h + c + 1, 1 - c, h + c)
                    route(2 * h + c, c)

            normalise(0, 0, 0)
            body(0)
            with dve.Fori(1, B // 2 - 1) as h:
                body(h)
            body(B // 2 - 1, last=True)

            dve.wait_ge(s_tot, 1)
            prep(nc.vector.tensor_copy(cnt[:], psR[:, 0, 0:E]))
            prep(nc.vector.tensor_scalar(cnti[:], cnt[:], float(P - 1), None, ALU.add))
            prep(nc.vector.tensor_single_scalar(cnti[:], cnti[:], 7, ALU.arith_shift_right))
            prep(nc.vector.tensor_copy(tiles[:], cnti[:]))
            prep(nc.vector.tensor_copy(acc[:, 0, :], tiles[:]))
            a, sh = 0, 1
            while sh < E:
                nc.vector.tensor_copy(acc[:, 1 - a, 0:sh], acc[:, a, 0:sh])
                prep(nc.vector.tensor_tensor(acc[:, 1 - a, sh:E], acc[:, a, sh:E], acc[:, a, 0:E - sh], ALU.add))
                a, sh = 1 - a, 2 * sh
            ends = acc[:, a, :]
            prep(nc.vector.tensor_tensor(base1[:], ends, tiles[:], ALU.subtract))
            prep(nc.vector.tensor_scalar(base1[:], base1[:], float(P), 1.0, ALU.mult, ALU.add))
            prep(nc.vector.tensor_tensor(padn[:, 0, :], base1[:], cnt[:], ALU.add))
            prep(nc.vector.tensor_scalar(padn[:, 0, :], padn[:, 0, :], iota[:, 0:1], -1.0, ALU.add, ALU.add))
            prep(nc.vector.scalar_tensor_tensor(padn[:, 1, :], ends, float(P), padn[:, 0, :], ALU.mult, ALU.subtract))
            prep(nc.vector.tensor_scalar(padn[:, 1, :], padn[:, 1, :], 0.5, 1.0e6, ALU.is_lt, ALU.mult))
            prep(nc.vector.tensor_tensor(K.padslot[:, 0:E], padn[:, 0, :], padn[:, 1, :], ALU.add))
            prep(nc.vector.tensor_scalar(K.padslot[:, E:E + 1], ends[:, E - 1:E], float(P), iota[:, 0:1], ALU.mult, ALU.add))
            prep(nc.vector.tensor_tensor(tcmp[:], ends[:, None, :].broadcast_to((P, 4, E)),
                                         iota[:, 0:4, None].broadcast_to((P, 4, E)), ALU.is_le))
            prep(nc.vector.tensor_reduce(ttab[:, 0, :], tcmp[:], AX.X, ALU.add))
            prep(nc.vector.tensor_scalar(ttab[:, 0, :], ttab[:, 0, :], float(E - 1), float(D), ALU.min, ALU.mult))
            prep(nc.vector.tensor_scalar(cnti[:, 0:1], acc[:, a, E - 1:E], 1.0, None, ALU.add))
            prep(nc.vector.tensor_single_scalar(cnti[:, 0:1], cnti[:, 0:1], 1, ALU.arith_shift_right))
            prep(nc.vector.tensor_copy(acc[:, 1 - a, 1:2], cnti[:, 0:1]))
            prep(nc.vector.tensor_scalar(acc[:, 1 - a, 0:1], acc[:, 1 - a, 1:2], -1.0, None, ALU.add))
            prep(nc.vector.tensor_scalar(ttab[:, 1, :], iota[:, 0:4], acc[:, 1 - a, 0:1], None, ALU.min))
            nc.vector.tensor_copy(ttabi[:], ttab[:]).then_inc(s_tt, 1)
            prep(nc.vector.tensor_tensor(slot[:], slot[:], base1[:, None, :].broadcast_to((P, NT, E)), ALU.add))
            prep(nc.vector.tensor_tensor(slot[:], slot[:], selall[:], ALU.mult))
            for t in range(NT):
                ins = nc.vector.max(top8[:, t, :], slot[:, t, :])
            prep(ins)
            prep(nc.vector.tensor_scalar(K.slots[:], top8[:, :, 0:TOPK], -1.0, None, ALU.add))
            for b in range(B):
                tb = slice(TB * b, TB * b + TB)
                prep(nc.vector.tensor_tensor(eqw[:], slot[:, tb, None, :].broadcast_to((P, TB, TOPK, E)),
                                             top8[:, tb, 0:TOPK, None].broadcast_to((P, TB, TOPK, E)), ALU.is_equal))
                prep(nc.vector.tensor_tensor(eqw[:], eqw[:], comb[:, tb, None, :].broadcast_to((P, TB, TOPK, E)), ALU.mult))
                prep(nc.vector.tensor_reduce(K.weights[:, tb, :], eqw[:], AX.X, ALU.add))


def load_expert_weights(nc, gate_upT, downT, tab_d, K, W, ident, identf):
    with ExitStack() as ctx:
        s_w = ctx.enter_context(nc.semaphore("expert_weights_loaded"))
        block = ctx.enter_context(nc.Block())

        @block.scalar
        def _(act):
            act.dma_start(W.gate_up[:].rearrange("p k e n -> p (k e n)"), gate_upT.rearrange("p k e n -> p (k e n)")).then_inc(s_w, 16)
            act.dma_start(W.down[:].rearrange("p e n -> p (e n)"), downT.rearrange("p e n -> p (e n)")).then_inc(s_w, 16)
            act.dma_start(identf[:], ident).then_inc(s_w, 16)
            act.dma_start(K.tables[0:1, :, :].rearrange("p w i -> p (w i)"), tab_d.rearrange("(o w) i -> o (w i)", o=1)).then_inc(s_w, 16)
            act.wait_ge(s_w, 64)


def experts(nc, xs_d, y_d, K, W, identf):
    R = 4
    N = SLOT_TILES // 2
    assert N % R == 0
    ctx = ExitStack()
    with ctx:
        sb = lambda n, s, d: ctx.enter_context(nc.sbuf_tensor(n, s, d))
        ps = lambda n, s, d: ctx.enter_context(nc.psum_tensor(n, s, d))
        sem = lambda n: ctx.enter_context(nc.semaphore(n))
        xrow = sb("xrow", [P, R, 2, D], F32)
        xT = sb("xT1", [P, 2, 2, KD, P], F32)
        gate = sb("gate", [P, 2, 2, I], F32)
        hid = sb("hid", [P, 2, 2, I], F32)
        hT = sb("hT", [P, 2, 2, P], F32)
        yrow = sb("yrow", [P, R, 2, D], F32)
        psX = ps("psX", [P, 2, S], F32)
        psG = ps("psG", [P, 2, 2, 2 * I], F32)
        psH = ps("psH", [P, 2, S], F32)
        psY = ps("psY", [P, 2, S], F32)
        s_xl = [sem(f"xrows_loaded{j}") for j in range(R)]
        s_ys = [sem(f"yrows_stored{j}") for j in range(R)]
        s_xtr = sem("x_transposed")
        s_xT = sem("xT_in_sbuf")
        s_gu = sem("gate_up_ready")
        s_g = sem("gate_silu_ready")
        s_h = sem("hidden_ready")
        s_htr = sem("hidden_transposed")
        s_hT = sem("hT_in_sbuf")
        s_y = sem("y_in_psum")
        s_yr = sem("y_in_sbuf")
        s_pass = sem("wait_passed_experts")
        xs_v = xs_d.rearrange("(q i p) n -> q p i n", p=P, i=2)
        y_v = y_d.rearrange("(q i p) n -> q p i n", p=P, i=2)
        w_up = [W.gate_up[:, k].rearrange("p e n -> p (e n)") for k in range(KD)]
        w_down = W.down[:].rearrange("p e n -> p (e n)")
        block = ctx.enter_context(nc.Block())

        def turns(engine, turn, begin=lambda g: None):
            for s in range(0, 2 * R):
                if s % R == 0:
                    begin(s // R)
                turn(s, s // R, s % R, lambda d, s=s: s >= d)
            with engine.Fori(2, N // R) as g:
                begin(g)
                for j in range(R):
                    turn(R * g + j, g, j, lambda d: True)
            begin(N // R)
            for s in range(N, N + 4):
                turn(s, s // R, s % R, lambda d, s=s: s - d < N)

        def fills(g, j, back):
            return g + 1 if j >= back else g

        def later(t, n):
            return not isinstance(t, int) or t >= n

        @block.sync
        def _(sp):
            rows = {}

            def begin(g):
                if not (isinstance(g, int) and g >= N // R):
                    rows["pair"] = nc.values_load_multi_w_load_instructions(
                        K.tables[0:1, 1, bass.ds(R * g, R)], engines=(mybir.EngineType.SP,), min_val=0, max_val=N - 1,
                        skip_runtime_bounds_check_because="the table is clamped")[1]

            def turn(s, g, j, has):
                if has(0):
                    t = rows["pair"][j]
                    if later(s, R):
                        sp.wait_ge(s_xtr, s - R + 1)
                        sp.sem_inc(s_pass, 1)
                    sp.dma_start(xrow[:, j], xs_v[bass.ds(t, 1)].rearrange("o p i n -> p (o i) n")).then_inc(s_xl[j], 16)
                if has(4):
                    y = s - 4
                    sp.wait_ge(s_yr, y + 1)
                    sp.sem_inc(s_pass, 1)
                    sp.dma_start(y_v[bass.ds(y, 1)].rearrange("o p i n -> p (o i) n"), yrow[:, j]).then_inc(s_ys[j], 16)
            turns(sp, turn, begin)
            for j in range(R):
                sp.wait_ge(s_ys[j], 16 * (N // R))

        @block.tensor
        def _(pe):
            cols = {}

            def begin(g):
                first = 2 * R * g - 6
                if isinstance(g, int):
                    lo, hi = max(first, 0), min(2 * R * g + 2 * R - 2, 2 * N)
                else:
                    lo, hi = first, first + 2 * R + 4
                n = hi - lo if isinstance(g, int) else 2 * R + 4
                v = nc.values_load_multi_w_load_instructions(
                    K.tables[0:1, 0, bass.ds(lo, n)], engines=(mybir.EngineType.PE,), min_val=0, max_val=(E - 1) * D,
                    skip_runtime_bounds_check_because="the table is clamped")[1]
                cols["at"] = lambda back_tiles: v[back_tiles + ((first - lo) if isinstance(g, int) else 0)]

            def column(j, back, i):
                return cols["at"](2 * (j - back) + i + 6)

            def turn(s, g, j, has):
                c = j % 2
                if has(0):
                    pe.wait_ge(s_xl[j], 16 * fills(g, j, 0))
                    if later(s, 2):
                        pe.wait_ge(s_xT, s - 1)
                    for i in range(2):
                        for k in range(KD):
                            at = P * (KD * i + k)
                            ins = nc.tensor.transpose(psX[:, c, at:at + P], xrow[:, j, i, P * k:P * k + P], identf[:])
                    ins.then_inc(s_xtr, 1)
                if has(1):
                    t, d = s - 1, 1 - c
                    pe.wait_ge(s_xT, t + 1)
                    if later(t, 2):
                        pe.wait_ge(s_h, t - 1)
                    for i in range(2):
                        e = column(j, 1, i)
                        for k in range(KD):
                            ins = nc.tensor.matmul(psG[:, d, i, :], xT[:, d, i, k, :], w_up[k][:, bass.ds(e, 2 * I)],
                                                   start=(k == 0), stop=(k == KD - 1))
                    ins.then_inc(s_gu, 1)
                if has(2):
                    t, d = s - 2, c
                    pe.wait_ge(s_h, t + 1)
                    if later(t, 2):
                        pe.wait_ge(s_hT, t - 1)
                    for i in range(2):
                        ins = nc.tensor.transpose(psH[:, d, P * i:P * i + P], hid[:, d, i, :], identf[:])
                    ins.then_inc(s_htr, 1)
                if has(3):
                    t, d = s - 3, 1 - c
                    pe.wait_ge(s_hT, t + 1)
                    if later(t, 2):
                        pe.wait_ge(s_yr, t - 1)
                    for i in range(2):
                        e = column(j, 3, i)
                        ins = nc.tensor.matmul(psY[:, d, D * i:D * i + D], hT[:, d, i, :], w_down[:, bass.ds(e, D)],
                                               start=True, stop=True)
                    ins.then_inc(s_y, 1)
            turns(pe, turn, begin)

        @block.scalar
        def _(act):
            def turn(s, g, j, has):
                c = j % 2
                if has(1):
                    t, d = s - 1, 1 - c
                    act.wait_ge(s_gu, t + 1)
                    if later(t, 2):
                        act.wait_ge(s_h, t - 1)
                    nc.scalar.activation(gate[:, d], psG[:, d, :, 0:I], ACT.Silu).then_inc(s_g, 1)
                if has(3):
                    t, d, r = s - 3, 1 - c, (j - 3) % R
                    act.wait_ge(s_y, t + 1)
                    if later(t, R):
                        act.wait_ge(s_ys[r], 16 * (fills(g, j, 3) - 1))
                    nc.scalar.copy(yrow[:, r].rearrange("p i n -> p (i n)"), psY[:, d, :]).then_inc(s_yr, 1)
            turns(act, turn)

        @block.vector
        def _(dve):
            def turn(s, g, j, has):
                c = j % 2
                if has(0):
                    dve.wait_ge(s_xtr, s + 1)
                    if later(s, 2):
                        dve.wait_ge(s_gu, s - 1)
                    nc.vector.tensor_copy(xT[:, c].rearrange("p i k n -> p (i k n)"), psX[:, c, :]).then_inc(s_xT, 1)
                if has(1):
                    t, d = s - 1, 1 - c
                    dve.wait_ge(s_g, t + 1)
                    if later(t, 2):
                        dve.wait_ge(s_htr, t - 1)
                    nc.vector.tensor_tensor(hid[:, d], gate[:, d], psG[:, d, :, I:2 * I], ALU.mult).then_inc(s_h, 1)
                if has(2):
                    t, d = s - 2, c
                    dve.wait_ge(s_htr, t + 1)
                    if later(t, 2):
                        dve.wait_ge(s_y, t - 1)
                    nc.vector.tensor_copy(hT[:, d].rearrange("p i n -> p (i n)"), psH[:, d, 0:2 * P]).then_inc(s_hT, 1)
            turns(dve, turn)


def combine(nc, part_d, y_d, out, K):
    R = 4
    ctx = ExitStack()
    with ctx:
        sb = lambda n, s, d: ctx.enter_context(nc.sbuf_tensor(n, s, d))
        sem = lambda n: ctx.enter_context(nc.semaphore(n))
        yk = sb("yk", [P, R, TOPK, D], F32)
        part = sb("part", [P, R, D], F32)
        idx = sb("idx2", [P, R, TOPK], U32)
        s_pl = [sem(f"part_loaded{j}") for j in range(R)]
        s_ix = sem("gather_indices_copied")
        s_gt = [sem(f"rows_gathered{j}") for j in range(R)]
        s_a = sem("sums_done")
        s_t = sem("tiles_summed")
        s_pass = sem("wait_passed_combine")
        s_o = [sem(f"out_stored{j}") for j in range(R)]
        part_v = part_d.rearrange("(t p) n -> t p n", p=P)
        out_v = out.rearrange("b (t p) n -> (b t) p n", p=P)
        block = ctx.enter_context(nc.Block())

        @block.sync
        def _(sp):
            for j in range(R):
                sp.dma_start(part[:, j, :], part_v[j]).then_inc(s_pl[j], 16)
            with sp.Fori(0, NT // R - 1) as g:
                for j in range(R):
                    t = R * g + j
                    sp.wait_ge(s_t, t + 1)
                    sp.dma_start(out_v[bass.ds(t, 1)].rearrange("o p n -> (o p) n"), part[:, j, :]).then_inc(s_o[j], 16)
                    sp.wait_ge(s_o[j], 16 * (g + 1))
                    sp.dma_start(part[:, j, :], part_v[bass.ds(t + R, 1)].rearrange("o p n -> (o p) n")).then_inc(s_pl[j], 16)
            for j in range(R):
                t = NT - R + j
                sp.wait_ge(s_t, t + 1)
                sp.dma_start(out_v[t], part[:, j, :]).then_inc(s_o[j], 16)
            for j in range(R):
                sp.wait_ge(s_o[j], 16 * (NT // R))

        @block.gpsimd
        def _(pool):
            def gather(g, j):
                t = R * g + j
                if not isinstance(g, int):
                    pool.wait_ge(s_gt[j], 16 * TOPK * g)
                nc.gpsimd.tensor_copy(idx[:, j, :], K.slots[:, bass.ds(t, 1), :].rearrange("p o k -> p (o k)")).then_inc(s_ix, 1)
                pool.wait_ge(s_ix, t + 1)
                if not isinstance(g, int):
                    pool.wait_ge(s_t, R * g - R + j + 1)
                pool.sem_inc(s_pass, 1)
                for k in range(TOPK):
                    nc.gpsimd.indirect_dma_start(yk[:, j, k, :], None, y_d,
                                                 bass.IndirectOffsetOnAxis(ap=idx[:, j, k:k + 1], axis=0)).then_inc(s_gt[j], 16)

            for j in range(R):
                gather(0, j)
            with pool.Fori(1, NT // R) as g:
                for j in range(R):
                    gather(g, j)

        @block.vector
        def _(dve):
            with dve.Fori(0, NT // R) as g:
                for j in range(R):
                    t = R * g + j
                    dve.wait_ge(s_pl[j], 16 * (g + 1))
                    dve.wait_ge(s_gt[j], 16 * TOPK * (g + 1))
                    for k in range(TOPK):
                        ins = nc.vector.scalar_tensor_tensor(part[:, j, :], yk[:, j, k, :],
                                                             K.weights[:, bass.ds(t, 1), k], part[:, j, :],
                                                             ALU.mult, ALU.add)
                        if k < TOPK - 1:
                            ins.then_inc(s_a, 1)
                            dve.wait_ge(s_a, (TOPK - 1) * t + k + 1)
                        else:
                            ins.then_inc(s_t, 1)



H, HD = 16, 16
HU = 8
NB = S // 32
NEG = -1.0e30
CAND = NB - 1 + 8
NCONST = 23


class Bank:

    def __init__(self, names, banks):
        self.bank = {x: i % banks for i, x in enumerate(names)}
        self.nth = {x: i // banks for i, x in enumerate(names)}
        self.uses = [sum(1 for i in range(len(names)) if i % banks == j) for j in range(banks)]

    def count(self, name, b):
        return self.uses[self.bank[name]] * b + self.nth[name] + 1


def attention(nc, x, xn_d, xs_d, part_d, A, K):
    qs_d = nc.dram_tensor("q_split", (2, 2, HU, HD, S), F32).ap()
    ks_d = nc.dram_tensor("k_split", (2, 2, HU, HD, S), F32).ap()
    sel_d = nc.dram_tensor("sel_bias", (2, HU, NB, S - P), F32).ap()
    ctx = ExitStack()
    with ctx:
        sb = lambda n, s, d: ctx.enter_context(nc.sbuf_tensor(n, s, d))
        ps = lambda n, s, d: ctx.enter_context(nc.psum_tensor(n, s, d))
        sem = lambda n: ctx.enter_context(nc.semaphore(n))

        identf = sb("ident_attn", [P, P], F32)
        cb = sb("const_b", [P, 4, P], BF16)
        ident_b, part_b, caus_qk, caus_kq = (cb[:, i, :] for i in range(4))
        cos = sb("cos", [P, S], F32)
        sin = sb("sin", [P, S], F32)
        force = sb("force", [P, TB - 1, NB], F32)
        edge = sb("edge", [P, TB - 1, NB], F32)
        hmask = sb("hmask", [P, HU], F32)
        wq = sb("wq", [P, KD, D], F32)
        wk = sb("wk", [P, KD, D], F32)
        wv = sb("wv", [P, KD, D], F32)
        wo = sb("wo", [P, KD, D], F32)
        wsg = sb("wsg", [P, KD, D], F32)
        wsu = sb("wsu", [P, KD, D], F32)
        wsd = sb("wsd", [P, KD, D], F32)
        lod = sb("lod", [P, 32, P], F32)

        xnb = sb("xnb", [P, TB, D], F32)
        xT = sb("xTa", [P, KD, S], F32)
        vsb = sb("vsb", [P, TB, H, 32], F32)
        th = sb("th", [P, S], F32)
        shT = sb("shT", [P, KD, S], F32)
        r1 = sb("r1", [P, S], F32)
        r2 = sb("r2", [P, S], F32)
        qf = sb("qf", [P, S], F32)
        kf = sb("kf", [P, S], F32)
        split = sb("split", [P, 4, S], F32R)
        qst = [sb(f"qst{c}", [P, HU, S], F32R) for c in range(2)]
        kst = [sb(f"kst{c}", [P, HU, S], F32R) for c in range(2)]
        k1bd = sb("k1bd", [P, HU, CAND], F32)
        top8 = sb("top8a", [P, 3 * HU, 8], F32)
        rep = sb("rep", [P, 3 * HU, CAND], F32)
        bias = sb("bias", [P, 3 * HU, NB], F32)
        sbias = sb("sbias", [P, 3 * HU, NB], F32)
        spart = sb("spart", [P, 3 * HU], F32)
        selT = sb("selT", [P, 3 * P], F32R)
        diag = sb("diag", [P, 2, 3 * HU, P], BF16)
        m = sb("m", [P, HU, TB], F32)
        mT = sb("mT", [HU // 2, 2, S], F32R)
        p0T = sb("p0T", [P, 2, 4, S], F32)
        p1T = sb("p1T", [P, 4, 3 * 2 * P], F32)
        oT = sb("oT", [P, S], F32)
        rs = sb("rs", [P, TB, 4], F32)
        on = sb("on", [P, TB, D], F32)
        oT2 = sb("oT2", [P, KD, S], F32)
        part = sb("part_a", [P, TB, D], F32)
        zeros = p0T[:, 0, 0, 0:D]
        idx = sb("idx", [P, TB, TOPK], U32)
        padi = sb("padi", [P, E + 1], U32)

        psA = ps("psA", [P, 2, S], F32)
        ps1 = ps("ps1", [P, 2, S], F32)
        ps2 = ps("ps2", [P, 2, S], F32)
        psO = ps("psO", [P, S], F32)
        psB = ps("psB", [P, S], F32)

        s_c = sem("a_consts_loaded")
        s_cv = sem("a_consts_ready")
        s_cz = sem("block_diagonal_cleared")
        s_pass = sem("wait_passed_attention")
        s_xb = sem("xn_loaded")
        s_xr = sem("residual_loaded")
        s_aR = [sem(f"a_bank_filled{j}") for j in range(2)]
        s_aF = [sem(f"a_bank_read{j}") for j in range(2)]
        s_1R = [sem(f"max_bank_filled{j}") for j in range(2)]
        s_1F = [sem(f"max_bank_read{j}") for j in range(2)]
        s_2R = [sem(f"exp_bank_filled{j}") for j in range(2)]
        s_2F = [sem(f"exp_bank_read{j}") for j in range(2)]
        s_bR = sem("b_bank_filled")
        s_bF = sem("b_bank_read")
        s_th = sem("tanh_ready")
        s_dv = sem("dve_step_a")
        s_q = sem("q_ready")
        s_k = sem("k_ready")
        s_wd = sem("split_stored")
        s_st = [sem(f"stack{c}_loaded") for c in range(2)]
        s_k1 = sem("k1_ready")
        s_sb = sem("sel_bias_ready")
        s_sp = sem("edge_bias_ready")
        s_sw = sem("selT_stored")
        s_sl = [sem(f"selT{c}_loaded") for c in range(2)]
        s_dg = sem("diag_ready")
        s_ml = [sem(f"max_rows{c}_loaded") for c in range(2)]
        s_pv = sem("pv_ready")
        s_oT = sem("oT_ready")
        s_ps = sem("part_stored")
        s_ix = sem("slot_indices_copied")
        s_z = sem("zeros_ready")
        s_sc = sem("rows_scattered")
        s_pad = sem("padding_zeroed")
        s_pass_s = sem("wait_passed_scatter")

        UNIT = ("K", "Q", "k1_", "sa", "sb", "sT")
        a = Bank(["xT0", "xT1"] + [f"{n}0" for n in UNIT] + ["K1", "Q1", "V0", "V1"] + [f"{n}1" for n in UNIT[2:]] + ["G0", "U0", "G1", "U1"], 2)
        bb = Bank([f"{n}_{c}" for c in range(2) for n in ("m0", "m1", "o0", "o1")] + ["t0", "t1", "y0", "y1"], 1)
        PAIR = [((3,), (0,)), ((3,), (1,)), ((2, 0), (0,)), ((2, 0), (1,)), ((1,), (0, 1))]
        GROUP2 = [((0,), (h,)) for h in range(4)] + [((1, 3), (h,)) for h in range(4)] + [((2,), (0, 1)), ((2,), (2, 3))]
        IT1 = [(tiles, tuple(2 * p + h for h in hs)) for p in range(HU // 2) for tiles, hs in PAIR]
        IT2 = [(tiles, tuple(4 * g + h for h in hs)) for g in range(2) for tiles, hs in GROUP2]
        NI = len(IT1)
        PCOL = [0, 0, S, 3 * P]

        x_v = x.rearrange("b (t p) n -> b p t n", p=P)
        xn_v = xn_d.rearrange("(b t p) n -> b p t n", t=TB, p=P)
        part_v = part_d.rearrange("(b t p) n -> b p t n", t=TB, p=P)
        block = ctx.enter_context(nc.Block())


        @block.sync
        def _(sp):
            sp.wait_ge(s_cz, 1)
            loads = [(identf[:], A.ident), (r1[:].rearrange("p (i n) -> p i n", i=4), A.masks), (cos[:], A.cos), (sin[:], A.sin), (force[:], A.force),
                     (edge[:], A.edge), (hmask[:], A.hmask), (th[64:82, :], A.krows)]
            loads += [(dst[:], src.rearrange("(k p) n -> p k n", p=P)) for dst, src in
                      ((wq, A.WqT), (wk, A.WkT), (wv, A.WvT), (wo, A.WoT), (wsg, A.sgT), (wsu, A.suT), (wsd, A.sdT))]
            loads += [(lod[HD * h:HD * h + HD, :, HD * h:HD * h + HD], A.lod1) for h in range(HU)]
            assert len(loads) == NCONST
            for dst, src in loads:
                sp.dma_start(dst, src).then_inc(s_c, 16)

            def tokens_in(b):
                if not isinstance(b, int) or b > 0:
                    sp.wait_ge(s_aR[a.bank["xT1"]], a.count("xT1", b - 1))
                    sp.wait_ge(s_sc, 16 * TB * TOPK * b)
                sp.dma_start(xnb[:], xn_v[bass.ds(b, 1)].rearrange("o p t n -> p (o t) n")).then_inc(s_xb, 16)

            def residual_in(b):
                sp.wait_ge(s_ps, 16 * b)
                sp.dma_start(part[:], x_v[bass.ds(b, 1)].rearrange("o p t n -> p (o t) n")).then_inc(s_xr, 16)

            def part_out(b):
                sp.wait_ge(s_bF, bb.count("y1", b))
                sp.dma_start(part_v[bass.ds(b, 1)].rearrange("o p t n -> p (o t) n"), part[:]).then_inc(s_ps, 16)

            def split_out(u, c, j):
                sp.wait_ge((s_q, s_k)[j], u + 1)
                for i in range(2):
                    sp.dma_start((qs_d, ks_d)[j][c, i].rearrange("h d t -> (h d) t"), split[:, 2 * j + i, :].bitcast(F32)).then_inc(s_wd, 16)

            def stacks_in(u, c):
                sp.wait_ge(s_wd, 64 * u + 64)
                if not isinstance(u, int) or u >= 2:
                    sp.wait_ge(s_pv, 2 * u - 2)
                sp.sem_inc(s_pass, 1)
                for r in range(4):
                    sp.dma_start(qst[c][HD * r:HD * r + HD].bitcast(F32), qs_d[c, r % 2].rearrange("h d t -> d h t")).then_inc(s_st[c], 16)
                    sp.dma_start(kst[c][HD * r:HD * r + HD].bitcast(F32), ks_d[c, r // 2].rearrange("h d t -> d h t")).then_inc(s_st[c], 16)

            def selection_in(b, u, c):
                sp.wait_ge(s_aF[a.bank[f"sT{c}"]], a.count(f"sT{c}", b))
                sp.dma_start(sel_d[c].rearrange("h j t -> (h j) t"), selT[:].bitcast(F32)).then_inc(s_sw, 16)
                sp.wait_ge(s_sw, 16 * u + 16)
                sp.dma_start(qst[c][64:80, :, P:S].bitcast(F32), sel_d[c].rearrange("h j t -> j h t")).then_inc(s_sl[c], 16)

            def maxima_in(b, c, g):
                sp.wait_ge(s_bF, bb.count(f"m{g}_{c}", b))
                for i in range(2):
                    sp.dma_start(qst[c][80 + i:81 + i, 4 * g:4 * g + 4, :].bitcast(F32), mT[:, i, :].bitcast(F32)).then_inc(s_ml[c], 16)

            def sequence(b, first, last):
                if not last:
                    tokens_in(b + 1)
                if not first:
                    part_out(b - 1)
                residual_in(b)
                maxima_in(b, 0, 0)
                maxima_in(b, 0, 1)
                selection_in(b, 2 * b + 1, 1)
                if not last:
                    split_out(2 * b + 2, 0, 1)
                maxima_in(b, 1, 0)
                if not last:
                    split_out(2 * b + 2, 0, 0)
                    stacks_in(2 * b + 2, 0)
                maxima_in(b, 1, 1)
                if not last:
                    selection_in(b + 1, 2 * b + 2, 0)
                    split_out(2 * b + 3, 1, 1)
                    split_out(2 * b + 3, 1, 0)
                    stacks_in(2 * b + 3, 1)

            tokens_in(0)
            split_out(0, 0, 1)
            split_out(0, 0, 0)
            stacks_in(0, 0)
            selection_in(0, 0, 0)
            split_out(1, 1, 1)
            split_out(1, 1, 0)
            stacks_in(1, 1)
            sequence(0, True, False)
            with sp.Fori(1, B - 1) as b:
                sequence(b, False, False)
            sequence(B - 1, False, True)
            part_out(B - 1)
            sp.wait_ge(s_ps, 16 * B)

        @block.gpsimd
        def _(pool):
            nc.gpsimd.tensor_copy(padi[:], K.padslot[:]).then_inc(s_ix, 1)
            pool.wait_ge(s_ix, 1)
            pool.wait_ge(s_z, 1)
            for e in range(E + 1):
                nc.gpsimd.indirect_dma_start(xs_d, bass.IndirectOffsetOnAxis(ap=padi[:, e:e + 1], axis=0), zeros, None,
                                             bounds_check=SLOT_TILES * P - 1, oob_is_err=False).then_inc(s_pad, 16)

            def scatter(b):
                pool.wait_ge(s_sc, 16 * TB * TOPK * b)
                nc.gpsimd.tensor_copy(idx[:].rearrange("p t k -> p (t k)"),
                                      K.slots[:, bass.ds(TB * b, TB), :].rearrange("p t k -> p (t k)")).then_inc(s_ix, 1)
                pool.wait_ge(s_ix, b + 2)
                pool.wait_ge(s_xb, 16 * b + 16)
                pool.sem_inc(s_pass_s, 1)
                for t in range(TB):
                    for k in range(TOPK):
                        nc.gpsimd.indirect_dma_start(xs_d, bass.IndirectOffsetOnAxis(ap=idx[:, t, k:k + 1], axis=0),
                                                     xnb[:, t, :], None).then_inc(s_sc, 16)

            scatter(0)
            with pool.Fori(1, B) as b:
                scatter(b)
            pool.wait_ge(s_sc, 16 * TB * TOPK * B)
            pool.wait_ge(s_pad, 16 * (E + 1))

        @block.tensor
        def _(pe):
            pe.wait_ge(s_c, 16 * NCONST)
            pe.wait_ge(s_cv, 1)

            def fill(name, b):
                j = a.bank[name]
                pe.wait_ge(s_aF[j], a.count(name, b) - 1)
                return psA[:, j, :], s_aR[j]

            def project(name, b, w, cols):
                o, ready = fill(name, b)
                for k in range(KD):
                    ins = nc.tensor.matmul(o, w[:, k, cols:cols + P], xT[:, k, :], start=(k == 0), stop=(k == KD - 1))
                ins.then_inc(ready, 1)

            def tokens_in(b):
                pe.wait_ge(s_xb, 16 * b + 16)
                for k in range(KD):
                    o, ready = fill(f"xT{k}", b)
                    for t in range(TB):
                        ins = nc.tensor.transpose(o[:, P * t:P * t + P], xnb[:, t, P * k:P * k + P], identf[:])
                    ins.then_inc(ready, 1)

            def values(b):
                for v in range(2):
                    o, ready = fill(f"V{v}", b)
                    for t in range(2):
                        for k in range(KD):
                            ins = nc.tensor.matmul(o[:, D * t:D * t + D], xT[:, k, P * (2 * v + t):P * (2 * v + t) + P], wv[:, k, :],
                                                   start=(k == 0), stop=(k == KD - 1))
                    ins.then_inc(ready, 1)

            def keys_queries(b, c):
                for k in range(KD):
                    pe.wait_ge(s_aF[a.bank[f"xT{k}"]], a.count(f"xT{k}", b))
                project(f"K{c}", b, wk, P * c)
                project(f"Q{c}", b, wq, P * c)

            def block_keys(b, c):
                pe.wait_ge(s_k, 2 * b + c + 1)
                o, ready = fill(f"k1_{c}", b)
                for g in range(32):
                    ins = nc.tensor.matmul(o[:, 0:NB], lod[:, g, :], kf[:].rearrange("p (n g) -> p g n", g=32)[:, g, :],
                                           start=(g == 0), stop=(g == 31))
                ins.then_inc(ready, 1)

            def block_scores(b, c):
                u = 2 * b + c
                pe.wait_ge(s_q, u + 1)
                pe.wait_ge(s_k1, u + 1)
                for name, tiles in (("sa", (1, 2)), ("sb", (3,))):
                    o, ready = fill(f"{name}{c}", b)
                    for i, t in enumerate(tiles):
                        ins = nc.tensor.matmul(o[:, i * HU * CAND:(i + 1) * HU * CAND], qf[:, P * t:P * t + P],
                                               k1bd[:].rearrange("p h j -> p (h j)"), start=True, stop=True)
                    ins.then_inc(ready, 1)

            def selection(b, c):
                pe.wait_ge(s_sb, 2 * b + c + 1)
                o, ready = fill(f"sT{c}", b)
                for t in range(3):
                    ins = nc.tensor.transpose(o[:, P * t:P * t + P],
                                              sbias[:, HU * t:HU * t + HU, :].rearrange("p h j -> p (h j)"), identf[:])
                ins.then_inc(ready, 1)

            def attend(b, c, beside):
                u = 2 * b + c
                beside(-1)
                pe.wait_ge(s_st[c], 128 * b + 128)
                pe.wait_ge(s_sl[c], 16 * b + 16)
                pe.wait_ge(s_dg, u + 1)

                def max_rows(g):
                    for j in range(2):
                        pe.wait_ge(s_1F[j], (NI // 2) * u + (NI // 4) * (g + 1))
                    pe.wait_ge(s_bF, bb.count(f"m{g}_{c}", b) - 1)
                    for t in range(TB):
                        ins = nc.tensor.transpose(psB[0:4, P * t:P * t + P], m[:, 4 * g:4 * g + 4, t], identf[:])
                    ins.then_inc(s_bR, 1)

                for i, (tiles, heads) in enumerate(IT1):
                    j = i % 2
                    pe.wait_ge(s_1F[j], (NI // 2) * u + i // 2)
                    at = 0
                    for h in heads:
                        for t in tiles:
                            n = P * (t + 1)
                            nc.tensor.matmul(ps1[:, j, at:at + n], qst[c][0:80, h, P * t:P * t + P], kst[c][0:80, h, 0:n],
                                             start=True, stop=False)
                            if t > 0:
                                nc.tensor.matmul(ps1[:, j, at + n - 2 * P:at + n - P], diag[:, c, HU * (t - 1) + h, :], part_b,
                                                 start=False, stop=False)
                            ins = nc.tensor.matmul(ps1[:, j, at + n - P:at + n], ident_b, caus_qk, start=False, stop=True)
                            at += n
                    ins.then_inc(s_1R[j], 1)
                    if i == 12:
                        max_rows(0)
                    beside(i)

                def scores(lo, hi):
                    for i in range(lo, hi):
                        tiles, heads = IT2[i]
                        j = i % 2
                        if i in (0, 10):
                            pe.wait_ge(s_ml[c], 64 * b + 32 * (i // 10 + 1))
                        pe.wait_ge(s_2F[j], (NI // 2) * u + i // 2)
                        at = 0
                        for h in heads:
                            for t in tiles:
                                n = S - P * t
                                nc.tensor.matmul(ps2[:, j, at:at + n], kst[c][0:82, h, P * t:P * t + P], qst[c][0:82, h, P * t:S],
                                                 start=True, stop=False)
                                if t < TB - 1:
                                    nc.tensor.matmul(ps2[:, j, at + P:at + 2 * P], part_b, diag[:, c, HU * t + h, :],
                                                     start=False, stop=False)
                                ins = nc.tensor.matmul(ps2[:, j, at:at + P], ident_b, caus_kq, start=False, stop=True)
                                at += n
                        ins.then_inc(s_2R[j], 1)
                        if i == 2:
                            max_rows(1)
                        beside(20 + i)

                def times_v(g):
                    for j in range(2):
                        pe.wait_ge(s_2F[j], (NI // 2) * u + 5 * (g + 1))
                    if c == 0 and g == 0:
                        for v in range(2):
                            pe.wait_ge(s_aF[a.bank[f"V{v}"]], a.count(f"V{v}", b))
                    pe.wait_ge(s_oT, 2 * u + g)
                    for t in range(TB):
                        for hh in range(4):
                            p = p0T[:, g, hh, :] if t == 0 else p1T[:, hh, PCOL[t]:PCOL[t] + S - P * t]
                            ins = nc.tensor.matmul(psO[32 * hh:32 * hh + 32, P * t:S], vsb[:, t, HU * c + 4 * g + hh, :],
                                                   p, start=(t == 0), stop=(t == TB - 1), skip_group_check=True)
                    ins.then_inc(s_pv, 1)

                def to_rows(g):
                    pe.wait_ge(s_oT, 2 * u + g + 1)
                    pe.wait_ge(s_bF, bb.count(f"o{g}_{c}", b) - 1)
                    for t in range(TB):
                        ins = nc.tensor.transpose(psB[:, P * t:P * t + P], oT[:, P * t:P * t + P], identf[:])
                    ins.then_inc(s_bR, 1)

                scores(0, 14)
                times_v(0)
                scores(14, 20)
                to_rows(0)
                times_v(1)
                to_rows(1)

            def output_columns(b, k):
                if k == 0:
                    pe.wait_ge(s_bF, bb.count("o1_1", b))
                pe.wait_ge(s_bF, bb.count(f"t{k}", b) - 1)
                for t in range(TB):
                    ins = nc.tensor.transpose(psB[:, P * t:P * t + P], on[:, t, P * k:P * k + P], identf[:])
                ins.then_inc(s_bR, 1)

            def output(b, v):
                if v == 0:
                    pe.wait_ge(s_bF, bb.count("t1", b))
                    pe.wait_ge(s_aF[a.bank["G1"]], a.count("G1", b))
                pe.wait_ge(s_bF, bb.count(f"y{v}", b) - 1)
                for t in range(2):
                    tok = P * (2 * v + t)
                    for k in range(KD):
                        nc.tensor.matmul(psB[:, D * t:D * t + D], oT2[:, k, tok:tok + P], wo[:, k, :], start=(k == 0), stop=False)
                    for k in range(KD):
                        ins = nc.tensor.matmul(psB[:, D * t:D * t + D], shT[:, k, tok:tok + P], wsd[:, k, :],
                                               start=False, stop=(k == KD - 1))
                ins.then_inc(s_bR, 1)

            def sequence(b, first, last):
                def beside0(turn):
                    if turn == -1:
                        values(b)
                        block_keys(b, 1)
                    if turn == 1:
                        block_scores(b, 1)
                    if turn in (2, 4) and not first:
                        output_columns(b - 1, turn // 2 - 1)
                    if turn in (6, 8) and not first:
                        output(b - 1, turn // 2 - 3)
                    if turn == 37:
                        selection(b, 1)

                def beside1(turn):
                    if turn in (-1, 1):
                        i = (turn + 1) // 2
                        project(f"G{i}", b, wsg, P * i)
                        project(f"U{i}", b, wsu, P * i)
                    if not last:
                        if turn == 4:
                            tokens_in(b + 1)
                        if turn == 6:
                            keys_queries(b + 1, 0)
                        if turn == 14:
                            block_keys(b + 1, 0)
                        if turn == 18:
                            block_scores(b + 1, 0)
                        if turn == 35:
                            selection(b + 1, 0)
                            keys_queries(b + 1, 1)

                attend(b, 0, beside0)
                attend(b, 1, beside1)

            tokens_in(0)
            keys_queries(0, 0)
            block_keys(0, 0)
            block_scores(0, 0)
            selection(0, 0)
            keys_queries(0, 1)
            sequence(0, True, False)
            with pe.Fori(1, B - 1) as b:
                sequence(b, False, False)
            sequence(B - 1, False, True)
            for k in range(KD):
                output_columns(B - 1, k)
            for v in range(2):
                output(B - 1, v)

        @block.scalar
        def _(act):
            def filled(name, b):
                j = a.bank[name]
                act.wait_ge(s_aR[j], a.count(name, b))
                return psA[:, j, :], s_aF[j]

            def tokens_in(b):
                for j in range(2):
                    act.wait_ge(s_aR[j], a.uses[j] * b)
                for k in range(KD):
                    o, free = filled(f"xT{k}", b)
                    nc.scalar.copy(xT[:, k, :], o).then_inc(free, 1)

            def values(b):
                act.wait_ge(s_pv, 4 * b)
                for v in range(2):
                    o, free = filled(f"V{v}", b)
                    for t in range(2):
                        ins = nc.scalar.copy(vsb[:, 2 * v + t, :, 0:HD],
                                             o[:, D * t:D * t + D].rearrange("p (h d) -> p h d", h=H))
                    ins.then_inc(free, 1)

            def gate(b, i):
                o, _ = filled(f"G{i}", b)
                if i == 0:
                    act.wait_ge(s_aF[a.bank["U1"]], a.uses[a.bank["U1"]] * b)
                else:
                    act.wait_ge(s_aF[a.bank["U0"]], a.count("U0", b))
                nc.scalar.activation(th[:], o, ACT.Tanh, scale=0.5).then_inc(s_th, 1)

            def selection(b, c):
                u = 2 * b + c
                o, free = filled(f"sT{c}", b)
                act.wait_ge(s_sw, 16 * u)
                nc.scalar.copy(selT[:], o[:, 0:3 * P]).then_inc(free, 1)

            def diagonals(b, c, lo, hi):
                u = 2 * b + c
                act.wait_ge(s_sp, u + 1)
                if not isinstance(u, int) or u >= 2:
                    act.wait_ge(s_pv, 2 * u - 2)
                for i in range(lo, hi):
                    ins = nc.scalar.activation(diag[:, c, i, :], ident_b, ACT.Copy, scale=spart[:, i:i + 1])
                if hi == 3 * HU:
                    ins.then_inc(s_dg, 1)

            def copy_out(b, c, g):
                act.wait_ge(s_pv, 4 * b + 2 * c + g + 1)
                act.wait_ge(s_bR, bb.count(f"o{g}_{c}", b) - 1)
                nc.scalar.copy(oT[:], psO[:]).then_inc(s_oT, 1)

            def attend(b, c, beside):
                u = 2 * b + c
                beside(-1)
                for i, (tiles, heads) in enumerate(IT2):
                    j, g = i % 2, i // 10
                    if i % 10 == 0 and (not isinstance(u, int) or 2 * u + g > 0):
                        act.wait_ge(s_pv, 2 * u - 1 + g)
                    if i % 10 == 4:
                        act.wait_ge(s_pv, 2 * u + g)
                    act.wait_ge(s_2R[j], (NI // 2) * u + i // 2 + 1)
                    h0 = heads[0] % 4
                    if len(heads) == 1:
                        out, src = (p0T[:, g, h0, :] if tiles == (0,) else p1T[:, h0, 0:S]), ps2[:, j, :]
                    else:
                        out = p1T[:, h0:h0 + 2, PCOL[2]:PCOL[2] + 2 * P]
                        src = ps2[:, j, :].rearrange("p (h n) -> p h n", h=2)
                    nc.scalar.activation(out, src, ACT.Exp, scale=float(HD) ** -0.5).then_inc(s_2F[j], 1)
                    if i == 14:
                        copy_out(b, c, 0)
                    beside(20 + i)
                copy_out(b, c, 1)
                beside(40)

            def output_columns(b, k):
                act.wait_ge(s_bR, bb.count(f"t{k}", b))
                nc.scalar.copy(oT2[:, k, :], psB[:]).then_inc(s_bF, 1)

            act.wait_ge(s_cv, 1)
            def sequence(b, first, last):
                def beside0(turn):
                    if turn == -1:
                        values(b)
                        if not first:
                            for k in range(KD):
                                output_columns(b - 1, k)
                    if turn == 37:
                        selection(b, 1)
                    if turn == 33:
                        diagonals(b, 1, 0, 2 * HU)
                    if turn == 40:
                        diagonals(b, 1, 2 * HU, 3 * HU)

                def beside1(turn):
                    if turn == -1:
                        for i in range(2):
                            gate(b, i)
                        if not last:
                            tokens_in(b + 1)
                    if turn == 35 and not last:
                        selection(b + 1, 0)
                    if turn == 33 and not last:
                        diagonals(b + 1, 0, 0, 2 * HU)
                    if turn == 40 and not last:
                        diagonals(b + 1, 0, 2 * HU, 3 * HU)

                attend(b, 0, beside0)
                attend(b, 1, beside1)

            tokens_in(0)
            selection(0, 0)
            diagonals(0, 0, 0, 3 * HU)
            act.wait_ge(s_pad, 16 * (E + 1))
            sequence(0, True, False)
            with act.Fori(1, B - 1) as b:
                sequence(b, False, False)
            sequence(B - 1, False, True)
            for k in range(KD):
                output_columns(B - 1, k)

        @block.vector
        def _(dve):
            nc.vector.memset(lod[:], 0.0).then_inc(s_cz, 1)
            nc.vector.memset(zeros, 0.0).then_inc(s_z, 1)
            dve.wait_ge(s_c, 16 * NCONST)
            for c in range(2):
                nc.vector.memset(qst[c][64:80, :, 0:P].bitcast(F32), 0.0)
                for h in range(HU):
                    nc.vector.tensor_copy(kst[c][64:82, h, :], th[64:82, :])
            nc.vector.memset(vsb[:, :, :, HD:HD + 1], 1.0)
            nc.vector.memset(vsb[:, :, :, HD + 1:32], 0.0)
            nc.vector.tensor_copy(cb[:].rearrange("p i n -> p (i n)"), r1[:]).then_inc(s_cv, 1)
            dve.wait_ge(s_cv, 1)
            cnt_ = [0]

            def count(ins):
                cnt_[0] += 1
                ins.then_inc(s_dv, 1)

            def settle(b):
                dve.wait_ge(s_dv, cnt_[0])

            def step(b, ins):
                count(ins)
                settle(b)

            def filled(name, b):
                j = a.bank[name]
                dve.wait_ge(s_aR[j], a.count(name, b))
                return psA[:, j, :], s_aF[j]

            def read(name, b):
                dve.wait_ge(s_aF[a.bank[name]], a.count(name, b))

            def shared(b, i):
                o, free = filled(f"U{i}", b)
                dve.wait_ge(s_th, 2 * b + i + 1)
                nc.vector.scalar_tensor_tensor(r1[:], th[:], 1.0, o, ALU.add, ALU.mult).then_inc(free, 1)
                read(f"U{i}", b)
                o, free = filled(f"G{i}", b)
                nc.vector.scalar_tensor_tensor(shT[:, i, :], r1[:], 0.5, o, ALU.mult, ALU.mult).then_inc(free, 1)
                read(f"G{i}", b)

            def rotate(b, c, name, dst, n, ready):
                u = 2 * b + c
                o, free = filled(f"{name}{c}", b)
                step(b, nc.vector.tensor_tensor(r1[:], o, cos[:], ALU.mult))
                nc.vector.tensor_tensor(r2[:], o, sin[:], ALU.mult).then_inc(free, 1)
                read(f"{name}{c}", b)
                dve.sem_inc(s_pass, 1)
                step(b, nc.vector.stream_shuffle(r2[:], r2[:], [(i // HD) * HD + (i + HD // 2) % HD for i in range(32)]))
                step(b, nc.vector.tensor_tensor(dst[:], r1[:], r2[:], ALU.add))
                if n == 2:
                    dve.wait_ge(s_wd, 64 * u)
                step(b, nc.vector.tensor_copy(split[:, n, :], dst[:]))
                nc.vector.tensor_tensor(split[:, n + 1, :], dst[:], split[:, n, :], ALU.subtract).then_inc(ready, 1)

            def block_keys(b, c):
                o, free = filled(f"k1_{c}", b)
                nc.vector.tensor_tensor(k1bd[:, :, 0:NB], o[:, None, 0:NB].broadcast_to((P, HU, NB)),
                                        hmask[:, :, None].broadcast_to((P, HU, NB)), ALU.mult).then_inc(free, 1)
                read(f"k1_{c}", b)
                nc.vector.tensor_copy(k1bd[:, :, NB:CAND], k1bd[:, :, NB - 1:NB].broadcast_to((P, HU, CAND - NB))).then_inc(s_k1, 1)

            def selection(b, c):
                u = 2 * b + c
                for name, tiles in (("sa", (0, 1)), ("sb", (2,))):
                    o, free = filled(f"{name}{c}", b)
                    cand = o[:, 0:len(tiles) * HU * CAND].rearrange("p (i j) -> p i j", j=CAND)
                    i0, n = HU * tiles[0], HU * len(tiles)
                    dve.sem_inc(s_pass, 1)
                    for i in range(n):
                        count(nc.vector.max(top8[:, i0 + i, :], cand[:, i, :]))
                    settle(b)
                    for i in range(n):
                        ins = nc.vector.match_replace(rep[:, i0 + i, :], top8[:, i0 + i, :], cand[:, i, :], -BIG)
                        if i < n - 1:
                            count(ins)
                    ins.then_inc(free, 1)
                    settle(b)
                    read(f"{name}{c}", b)
                step(b, nc.vector.tensor_scalar(bias[:], rep[:, :, 0:NB], -BIG, -NEG, ALU.is_equal, ALU.mult))
                step(b, nc.vector.tensor_scalar(bias[:], bias[:], NEG, None, ALU.add))
                nc.vector.tensor_tensor(sbias[:].rearrange("p (t h) j -> p t h j", h=HU), bias[:].rearrange("p (t h) j -> p t h j", h=HU),
                                        force[:, :, None, :].broadcast_to((P, 3, HU, NB)), ALU.max).then_inc(s_sb, 1)
                step(b, nc.vector.tensor_tensor(bias[:].rearrange("p (t h) j -> p t h j", h=HU), bias[:].rearrange("p (t h) j -> p t h j", h=HU),
                                                edge[:, :, None, :].broadcast_to((P, 3, HU, NB)), ALU.mult))
                dve.wait_ge(s_dg, u)
                nc.vector.tensor_reduce(spart[:], bias[:], AX.X, ALU.add).then_inc(s_sp, 1)
                dve.wait_ge(s_sp, u + 1)

            def attend(b, c, beside):
                u = 2 * b + c

                def max_rows(g):
                    dve.wait_ge(s_bR, bb.count(f"m{g}_{c}", b))
                    if g == 1:
                        dve.wait_ge(s_ml[c], 64 * b + 32)
                    elif c == 1:
                        dve.wait_ge(s_ml[0], 64 * b + 64)
                    else:
                        dve.wait_ge(s_ml[1], 64 * b)
                    step(b, nc.vector.tensor_scalar(mT[:, 0, :], psB[0:4, :], -1.0, None, ALU.mult))
                    nc.vector.scalar_tensor_tensor(mT[:, 1, :], psB[0:4, :], -1.0, mT[:, 0, :], ALU.mult, ALU.subtract).then_inc(s_bF, 1)

                beside(-1)
                for i, (tiles, heads) in enumerate(IT1):
                    j = i % 2
                    dve.wait_ge(s_1R[j], (NI // 2) * u + i // 2 + 1)
                    if len(heads) == 2:
                        ins = nc.vector.tensor_reduce(m[:, heads[0]:heads[0] + 2, 1], ps1[:, j, :].rearrange("p (h n) -> p h n", h=2),
                                                      AX.X, ALU.max)
                    else:
                        at = 0
                        for t in tiles:
                            n = P * (t + 1)
                            ins = nc.vector.tensor_reduce(m[:, heads[0], t:t + 1], ps1[:, j, at:at + n], AX.X, ALU.max)
                            at += n
                    ins.then_inc(s_1F[j], 1)
                    if i == 12:
                        max_rows(0)
                    beside(i)
                max_rows(1)
                beside(39)
                for g in range(2):
                    dve.wait_ge(s_bR, bb.count(f"o{g}_{c}", b))
                    o = psB[:].rearrange("p (t h d) -> p t h d", t=TB, h=4)
                    step(b, nc.vector.reciprocal(rs[:], o[:, :, :, HD]))
                    h0 = (HU * c + 4 * g) * HD
                    nc.vector.tensor_tensor(on[:, :, h0:h0 + 4 * HD].rearrange("p t (h d) -> p t h d", h=4), o[:, :, :, 0:HD],
                                            rs[:, :, :, None].broadcast_to((P, TB, 4, HD)), ALU.mult).then_inc(s_bF, 1)
                    dve.wait_ge(s_bF, bb.count(f"o{g}_{c}", b))

            def output(b, v):
                dve.wait_ge(s_xr, 16 * b + 16)
                dve.wait_ge(s_bR, bb.count(f"y{v}", b))
                nc.vector.tensor_tensor(part[:, 2 * v:2 * v + 2, :].rearrange("p t n -> p (t n)"),
                                        part[:, 2 * v:2 * v + 2, :].rearrange("p t n -> p (t n)"), psB[:], ALU.add).then_inc(s_bF, 1)

            def from_zero(b):
                settle(b)
                dve.sem_inc(s_pass, 1)
                dve.sem_clear(s_dv)
                cnt_[0] = 0

            def sequence(b, first, last):
                def beside0(turn):
                    if turn == -1:
                        block_keys(b, 1)
                    if turn in (7, 9) and not first:
                        output(b - 1, (turn - 7) // 2)
                    if turn == 39:
                        selection(b, 1)

                def beside1(turn):
                    if turn in (0, 3):
                        shared(b, turn // 3)
                    if not last:
                        if turn == 9:
                            rotate(b + 1, 0, "K", kf, 2, s_k)
                        if turn == 12:
                            rotate(b + 1, 0, "Q", qf, 0, s_q)
                        if turn == 16:
                            block_keys(b + 1, 0)
                        if turn == 39:
                            selection(b + 1, 0)
                            rotate(b + 1, 1, "K", kf, 2, s_k)
                            rotate(b + 1, 1, "Q", qf, 0, s_q)

                attend(b, 0, beside0)
                attend(b, 1, beside1)
                from_zero(b)

            rotate(0, 0, "K", kf, 2, s_k)
            rotate(0, 0, "Q", qf, 0, s_q)
            block_keys(0, 0)
            selection(0, 0)
            rotate(0, 1, "K", kf, 2, s_k)
            rotate(0, 1, "Q", qf, 0, s_q)
            from_zero(0)
            sequence(0, True, False)
            with dve.Fori(1, B - 1) as b:
                sequence(b, False, False)
            sequence(B - 1, False, True)
            for v in range(2):
                output(B - 1, v)


class Kept:
    pass


def program(nc, ins, out):
    xn_d = nc.dram_tensor("xn_d", (T, D), F32).ap()
    xs_d = nc.dram_tensor("xs_d", (SLOT_TILES * P, D), F32).ap()
    y_d = nc.dram_tensor("y_d", (SLOT_TILES * P, D), F32).ap()
    part_d = nc.dram_tensor("part_d", (T, D), F32).ap()
    tab_d = nc.dram_tensor("tab_d", (2, 4 * P), I32).ap()
    K, W, A = Kept(), Kept(), Kept()
    A.ident, A.masks, A.cos, A.sin, A.force, A.edge, A.hmask, A.krows = (
        ins[n] for n in ("ident", "masks", "cos", "sin", "force", "edge", "hmask", "krows"))
    A.WqT, A.WkT, A.WvT, A.WoT, A.sgT, A.suT, A.sdT, A.lod1 = (
        ins[n] for n in ("WqT", "WkT", "WvT", "WoT", "sgT", "suT", "sdT", "lod1"))
    with ExitStack() as ctx:
        sb = lambda n, s, d: ctx.enter_context(nc.sbuf_tensor(n, s, d))
        K.slots = sb("slots", [P, NT, TOPK], U32)
        K.weights = sb("weights", [P, NT, TOPK], F32)
        with ExitStack() as pctx:
            K.padslot = pctx.enter_context(nc.sbuf_tensor("padslot", [P, E + 1], U32))
            front(nc, ins["x"], ins["gate_wT"], ins["gate_bias"], ins["tri"], ins["ident"], ins["tok_iota"], xn_d, xs_d, tab_d, K)
            attention(nc, ins["x"], xn_d, xs_d, part_d, A, K)
        with ExitStack() as wctx:
            wsb = lambda n, s, d: wctx.enter_context(nc.sbuf_tensor(n, s, d))
            K.tables = wsb("tables", [P, 2, 4 * P], I32)
            identf = wsb("identf", [P, P], F32)
            W.gate_up = wsb("w_gate_up", [P, KD, E, 2 * I], F32)
            W.down = wsb("w_down", [P, E, D], F32)
            load_expert_weights(nc, ins["gate_upT"], ins["downT"], tab_d, K, W, ins["ident"], identf)
            experts(nc, xs_d, y_d, K, W, identf)
        combine(nc, part_d, y_d, out, K)


def laid_out(inputs):
    a = {k: np.ascontiguousarray(np.asarray(v)) for k, v in inputs.items()}
    c = np.ascontiguousarray
    one = np.ones((P, P), np.float32)
    r = np.arange(P)
    key, qry = r[None, :], r[:, None]
    inv = (1.0 / np.float32(10000.0) ** (np.arange(0, HD, 2, dtype=np.float32) / np.float32(HD))).astype(np.float32)
    ang = np.arange(S, dtype=np.float32)[None, :] * inv[r % (HD // 2)][:, None]
    sign = np.where(r % HD < HD // 2, 1.0, -1.0).astype(np.float32)[:, None]
    blk = (P * np.arange(1, TB)[None, :] + r[:, None]) // 32
    j = np.arange(NB)[None, None, :]
    eye = np.eye(P, dtype=np.float32)
    edge_keys = ((qry // 32 == key // 32) & (key % 32 <= qry % 32)).astype(np.float32)
    later = np.where(key > qry, np.float32(NEG), np.float32(0.0)).astype(np.float32)
    return {
        "x": a["L0_attn_x"],
        "gate_wT": c(a["L0_ffn_gate_weight"].T),
        "gate_bias": a["L0_ffn_e_score_correction_bias"].reshape(1, E),
        "gate_upT": c(a["L0_ffn_experts_gate_up"].reshape(E, 2 * I, KD, P).transpose(3, 2, 0, 1)),
        "downT": c(a["L0_ffn_experts_down"].transpose(2, 0, 1)),
        "tri": np.concatenate([np.triu(one, 1), one], axis=1),
        "ident": eye,
        "tok_iota": c((r.astype(np.float32)[:, None] + P * np.arange(5, dtype=np.float32)[None, :])),
        "WqT": c(a["L0_attn_W_q"].T), "WkT": c(a["L0_attn_W_k"].T), "WvT": c(a["L0_attn_W_v"].T), "WoT": c(a["L0_attn_W_o"].T),
        "sgT": c(a["L0_ffn_shared_gate_w"].T), "suT": c(a["L0_ffn_shared_up_w"].T), "sdT": c(a["L0_ffn_shared_down_w"].T),
        "lod1": c(a["L0_attn_k_lod1"].reshape(HD, 32, HD).transpose(2, 1, 0)),
        "masks": c(np.stack([eye, edge_keys, later, later.T], axis=1)),
        "cos": np.cos(ang), "sin": np.sin(ang) * sign,
        "force": c(np.where(j >= blk[:, :, None] - 4, np.float32(0.0), np.float32(NEG)).astype(np.float32)),
        "edge": c((j == blk[:, :, None] - 4).astype(np.float32)),
        "hmask": c((r[:, None] // HD == np.arange(HU)[None, :]).astype(np.float32)),
        "krows": c(np.concatenate([(np.arange(S)[None, :] // 32 == np.arange(NB)[:, None]).astype(np.float32),
                                   np.ones((2, S), np.float32)])),
    }


def kernel(**inputs):
    import concourse.bacc as _bacc
    from concourse.bass_utils import run_bass_kernel_spmd as _run

    nc = _bacc.Bacc("TRN2", target_bir_lowering=False, num_devices=1)
    arrays, args = {}, {}
    for name, a in laid_out(inputs).items():
        arrays[f"in_{name}"] = a
        args[name] = nc.dram_tensor(f"in_{name}", a.shape, mybir.dt.from_np(a.dtype), kind="ExternalInput").ap()
    out = nc.dram_tensor("out_0", (B, S, D), F32, kind="ExternalOutput").ap()
    program(nc, args, out)
    r = _run(nc, [arrays], core_ids=[0])
    return r.results[0]["out_0"]
```
